# Optimizing a Trainium2 kernel written in Bass

```python
import numpy as np
import jax
import jax.numpy as jnp

def _softmax(x, axis=-1):
    return jax.nn.softmax(x, axis=axis)

def _gelu(x):
    return jax.nn.gelu(x, approximate=True)

def _silu(x):
    return jax.nn.silu(x)

def _sigmoid(x):
    return jax.nn.sigmoid(x)

def _layernorm(x, axis=-1, eps=1e-05):
    m = jnp.mean(x, axis=axis, keepdims=True)
    v = jnp.var(x, axis=axis, keepdims=True)
    return (x - m) / jnp.sqrt(v + eps)

def _scatter_add(tgt, idx, src, axis=0):
    return tgt.at[idx].add(src)

def _segment_sum(src, seg, n):
    return jax.ops.segment_sum(src, seg, n)
kernel_name = 'mk_gnn_resnorm_d2_gnn_r32_482ac2'

def setup_inputs(seed: int=0):
    np.random.seed(seed)
    _w = jnp.asarray

    def _rec_inputs():
        import jax
        import jax.numpy as jnp
        _gk = jax.random.key(seed)
        x = 8.953e-05 + 1 * jax.random.normal(jax.random.fold_in(_gk, 1), (3125, 16), jnp.float32)
        _s = jax.random.randint(jax.random.fold_in(_gk, 2), (50000,), 0, 3125, jnp.int32)
        _d = jax.random.randint(jax.random.fold_in(_gk, 3), (50000,), 0, 3125, jnp.int32)
        _loop = jnp.arange(3125, dtype=jnp.int32)
        src = jnp.concatenate([_s, _d, _loop])
        dst = jnp.concatenate([_d, _s, _loop])
        _o = jnp.argsort(dst, stable=True)
        src = src[_o]
        dst = dst[_o]
        edge_attr_3 = -1.09012e-05 + 0.99985 * jax.random.normal(jax.random.fold_in(_gk, 11), (103125, 3), jnp.float32)
        edge_attr_48 = -3.69585e-06 + 0.999911 * jax.random.normal(jax.random.fold_in(_gk, 12), (103125, 48), jnp.float32)
        edge_type_8 = jax.random.randint(jax.random.fold_in(_gk, 14), (103125,), 0, 8, jnp.int32)
        return (x, src, dst, edge_attr_3, edge_attr_48, edge_type_8)
    x, src, dst, edge_attr_3, edge_attr_48, edge_type_8 = _rec_inputs()

    def _L0_gnn_setup():
        import jax, jax.numpy as jnp
        import numpy as np
        NS, NV = (16, 4)
        EPS = 1e-05
        N_NODES, N_EDGES = (1250, 12500)

        def _bn_scalar(x, g, b):
            m = x.mean(0)
            v = ((x - m) ** 2).mean(0)
            return (x - m) / jnp.sqrt(v + EPS) * g + b

        def _seg_mean(x, idx, n):
            s = jax.ops.segment_sum(x, idx, num_segments=n)
            c = jax.ops.segment_sum(jnp.ones((idx.shape[0],), x.dtype), idx, num_segments=n)
            return s / jnp.maximum(c, 1.0)[:, None]

        def _edge_weights(edge_attr, w1, b1, w2, b2):
            h = jax.nn.relu(edge_attr @ w1 + b1)
            return h @ w2 + b2

        def _forward(node_attr, edge_attr, edge_vec, fc0_w1, fc0_b1, fc0_w2, fc0_b2, fc1_w1, fc1_b1, fc1_w2, fc1_b2, bn0_gs, bn0_bs, bn0_gv, bn1_gs, bn1_bs, edge_index):
            N = node_attr.shape[0]
            E = edge_attr.shape[0]
            src, dst = (edge_index[0], edge_index[1])
            rhat = edge_vec / (jnp.linalg.norm(edge_vec, axis=-1, keepdims=True) + 1e-12)
            sh1 = rhat * float(np.sqrt(3.0))
            w = _edge_weights(edge_attr, fc0_w1, fc0_b1, fc0_w2, fc0_b2)
            wa = w[:, :NS * NS].reshape(E, NS, NS)
            wb = w[:, NS * NS:].reshape(E, NS, NV)
            x = node_attr[dst]
            inv = float(1.0 / np.sqrt(NS))
            msg_s = jnp.einsum('ei,eij->ej', x, wa) * inv
            msg_v = jnp.einsum('ei,eij,ec->ejc', x, wb, sh1) * inv
            msg = jnp.concatenate([msg_s, msg_v.reshape(E, NV * 3)], axis=-1)
            out = _seg_mean(msg, src, N)
            s0 = _bn_scalar(out[:, :NS], bn0_gs, bn0_bs)
            v0 = out[:, NS:].reshape(N, NV, 3)
            vn = jnp.sqrt((v0 ** 2).mean(axis=(0, 2)) + EPS)
            v0 = v0 / vn[None, :, None] * bn0_gv[None, :, None]
            w = _edge_weights(edge_attr, fc1_w1, fc1_b1, fc1_w2, fc1_b2)
            wa = w[:, :NS * NS].reshape(E, NS, NS)
            wb = w[:, NS * NS:].reshape(E, NV, NS)
            s = s0[dst]
            v = v0[dst]
            path_a = jnp.einsum('ei,eij->ej', s, wa)
            path_b = jnp.einsum('eic,ec,eij->ej', v, sh1, wb) * float(1.0 / np.sqrt(3.0))
            msg = (path_a + path_b) * float(1.0 / np.sqrt(NS + NV))
            node1 = _seg_mean(msg, src, N)
            return _bn_scalar(node1, bn1_gs, bn1_bs)
        key = jax.random.key(seed)
        ks = jax.random.split(key, 8)
        d = 3 * NS
        wn = NS * NS + NS * NV
        g = lambda k, shape, sc: jax.random.normal(k, shape, jnp.float32) * sc
        return {'node_attr': g(ks[0], (N_NODES, NS), 1.0), 'edge_attr': g(ks[1], (N_EDGES, d), 1.0), 'edge_vec': g(ks[2], (N_EDGES, 3), 1.0), 'fc0_w1': g(ks[3], (d, d), d ** (-0.5)), 'fc0_b1': jnp.zeros((d,), jnp.float32), 'fc0_w2': g(ks[4], (d, wn), d ** (-0.5)), 'fc0_b2': jnp.zeros((wn,), jnp.float32), 'fc1_w1': g(ks[5], (d, d), d ** (-0.5)), 'fc1_b1': jnp.zeros((d,), jnp.float32), 'fc1_w2': g(ks[6], (d, wn), d ** (-0.5)), 'fc1_b2': jnp.zeros((wn,), jnp.float32), 'bn0_gs': jnp.ones((NS,), jnp.float32), 'bn0_bs': jnp.zeros((NS,), jnp.float32), 'bn0_gv': jnp.ones((NV,), jnp.float32), 'bn1_gs': jnp.ones((NS,), jnp.float32), 'bn1_bs': jnp.zeros((NS,), jnp.float32), 'edge_index': jax.random.randint(ks[7], (2, N_EDGES), 0, N_NODES)}
    _L0_gnn_all = _L0_gnn_setup()
    _L0_gnn_in = {k: v for k, v in _L0_gnn_all.items() if k in ('fc0_w1', 'fc0_b1', 'fc0_w2', 'fc0_b2', 'fc1_w1', 'fc1_b1', 'fc1_w2', 'fc1_b2', 'bn0_gs', 'bn0_bs', 'bn0_gv', 'bn1_gs', 'bn1_bs')}
    del _L0_gnn_all

    def _L1_gnn_setup():
        import jax, jax.numpy as jnp
        import numpy as np
        N_NODES = 3125
        N_EDGES = 100000
        NUM_REL = 8

        def _rgcn_layer(x, src, dst, edge_type, W, root, bias):
            out = x @ root + bias
            x_src = x[src]
            for r in range(W.shape[0]):
                mask = (edge_type == r).astype(x.dtype)
                s = jax.ops.segment_sum(x_src * mask[:, None], dst, num_segments=x.shape[0])
                cnt = jax.ops.segment_sum(mask, dst, num_segments=x.shape[0])
                agg = s / jnp.clip(cnt, 1.0)[:, None]
                out = out + agg @ W[r]
            return out
        key = jax.random.key(seed)
        ks = jax.random.split(key, 9)
        x = jax.random.normal(ks[0], (N_NODES, 16), dtype=jnp.float32)
        edge_index = jax.random.randint(ks[1], (2, N_EDGES), 0, N_NODES, dtype=jnp.int32)
        edge_type = jax.random.randint(ks[2], (N_EDGES,), 0, NUM_REL, dtype=jnp.int32)
        s1 = 1.0 / np.sqrt(16.0)
        s2 = 1.0 / np.sqrt(32.0)
        W1 = jax.random.normal(ks[3], (NUM_REL, 16, 32), dtype=jnp.float32) * s1
        root1 = jax.random.normal(ks[4], (16, 32), dtype=jnp.float32) * s1
        b1 = jnp.zeros((32,), dtype=jnp.float32)
        W2 = jax.random.normal(ks[5], (NUM_REL, 32, 16), dtype=jnp.float32) * s2
        root2 = jax.random.normal(ks[6], (32, 16), dtype=jnp.float32) * s2
        b2 = jnp.zeros((16,), dtype=jnp.float32)
        return {'x': x, 'edge_index': edge_index, 'edge_type': edge_type, 'W1': W1, 'root1': root1, 'b1': b1, 'W2': W2, 'root2': root2, 'b2': b2}
    _L1_gnn_all = _L1_gnn_setup()
    _L1_gnn_in = {k: v for k, v in _L1_gnn_all.items() if k in ('W1', 'root1', 'b1', 'W2', 'root2', 'b2')}
    del _L1_gnn_all
    return {'x': x, 'src': src, 'dst': dst, 'edge_attr_3': edge_attr_3, 'edge_attr_48': edge_attr_48, 'edge_type_8': edge_type_8, 'L0_gnn_fc0_w1': _L0_gnn_in['fc0_w1'], 'L0_gnn_fc0_b1': _L0_gnn_in['fc0_b1'], 'L0_gnn_fc0_w2': _L0_gnn_in['fc0_w2'], 'L0_gnn_fc0_b2': _L0_gnn_in['fc0_b2'], 'L0_gnn_fc1_w1': _L0_gnn_in['fc1_w1'], 'L0_gnn_fc1_b1': _L0_gnn_in['fc1_b1'], 'L0_gnn_fc1_w2': _L0_gnn_in['fc1_w2'], 'L0_gnn_fc1_b2': _L0_gnn_in['fc1_b2'], 'L0_gnn_bn0_gs': _L0_gnn_in['bn0_gs'], 'L0_gnn_bn0_bs': _L0_gnn_in['bn0_bs'], 'L0_gnn_bn0_gv': _L0_gnn_in['bn0_gv'], 'L0_gnn_bn1_gs': _L0_gnn_in['bn1_gs'], 'L0_gnn_bn1_bs': _L0_gnn_in['bn1_bs'], 'L1_gnn_W1': _L1_gnn_in['W1'], 'L1_gnn_root1': _L1_gnn_in['root1'], 'L1_gnn_b1': _L1_gnn_in['b1'], 'L1_gnn_W2': _L1_gnn_in['W2'], 'L1_gnn_root2': _L1_gnn_in['root2'], 'L1_gnn_b2': _L1_gnn_in['b2']}

def reference(x, src, dst, edge_attr_3, edge_attr_48, edge_type_8, L0_gnn_fc0_w1, L0_gnn_fc0_b1, L0_gnn_fc0_w2, L0_gnn_fc0_b2, L0_gnn_fc1_w1, L0_gnn_fc1_b1, L0_gnn_fc1_w2, L0_gnn_fc1_b2, L0_gnn_bn0_gs, L0_gnn_bn0_bs, L0_gnn_bn0_gv, L0_gnn_bn1_gs, L0_gnn_bn1_bs, L1_gnn_W1, L1_gnn_root1, L1_gnn_b1, L1_gnn_W2, L1_gnn_root2, L1_gnn_b2):
    import jax
    import jax.numpy as jnp

    def _L0_gnn_ref(node_attr, edge_attr, edge_vec, fc0_w1, fc0_b1, fc0_w2, fc0_b2, fc1_w1, fc1_b1, fc1_w2, fc1_b2, bn0_gs, bn0_bs, bn0_gv, bn1_gs, bn1_bs, edge_index):
        import jax, jax.numpy as jnp
        import numpy as np
        NS, NV = (16, 4)
        EPS = 1e-05
        N_NODES, N_EDGES = (1250, 12500)

        def _bn_scalar(x, g, b):
            m = x.mean(0)
            v = ((x - m) ** 2).mean(0)
            return (x - m) / jnp.sqrt(v + EPS) * g + b

        def _seg_mean(x, idx, n):
            s = jax.ops.segment_sum(x, idx, num_segments=n)
            c = jax.ops.segment_sum(jnp.ones((idx.shape[0],), x.dtype), idx, num_segments=n)
            return s / jnp.maximum(c, 1.0)[:, None]

        def _edge_weights(edge_attr, w1, b1, w2, b2):
            h = jax.nn.relu(edge_attr @ w1 + b1)
            return h @ w2 + b2

        def _forward(node_attr, edge_attr, edge_vec, fc0_w1, fc0_b1, fc0_w2, fc0_b2, fc1_w1, fc1_b1, fc1_w2, fc1_b2, bn0_gs, bn0_bs, bn0_gv, bn1_gs, bn1_bs, edge_index):
            N = node_attr.shape[0]
            E = edge_attr.shape[0]
            src, dst = (edge_index[0], edge_index[1])
            rhat = edge_vec / (jnp.linalg.norm(edge_vec, axis=-1, keepdims=True) + 1e-12)
            sh1 = rhat * float(np.sqrt(3.0))
            w = _edge_weights(edge_attr, fc0_w1, fc0_b1, fc0_w2, fc0_b2)
            wa = w[:, :NS * NS].reshape(E, NS, NS)
            wb = w[:, NS * NS:].reshape(E, NS, NV)
            x = node_attr[dst]
            inv = float(1.0 / np.sqrt(NS))
            msg_s = jnp.einsum('ei,eij->ej', x, wa) * inv
            msg_v = jnp.einsum('ei,eij,ec->ejc', x, wb, sh1) * inv
            msg = jnp.concatenate([msg_s, msg_v.reshape(E, NV * 3)], axis=-1)
            out = _seg_mean(msg, src, N)
            s0 = _bn_scalar(out[:, :NS], bn0_gs, bn0_bs)
            v0 = out[:, NS:].reshape(N, NV, 3)
            vn = jnp.sqrt((v0 ** 2).mean(axis=(0, 2)) + EPS)
            v0 = v0 / vn[None, :, None] * bn0_gv[None, :, None]
            w = _edge_weights(edge_attr, fc1_w1, fc1_b1, fc1_w2, fc1_b2)
            wa = w[:, :NS * NS].reshape(E, NS, NS)
            wb = w[:, NS * NS:].reshape(E, NV, NS)
            s = s0[dst]
            v = v0[dst]
            path_a = jnp.einsum('ei,eij->ej', s, wa)
            path_b = jnp.einsum('eic,ec,eij->ej', v, sh1, wb) * float(1.0 / np.sqrt(3.0))
            msg = (path_a + path_b) * float(1.0 / np.sqrt(NS + NV))
            node1 = _seg_mean(msg, src, N)
            return _bn_scalar(node1, bn1_gs, bn1_bs)
        return _forward(node_attr, edge_attr, edge_vec, fc0_w1, fc0_b1, fc0_w2, fc0_b2, fc1_w1, fc1_b1, fc1_w2, fc1_b2, bn0_gs, bn0_bs, bn0_gv, bn1_gs, bn1_bs, edge_index)

    def _L1_gnn_ref(x, edge_index, edge_type, W1, root1, b1, W2, root2, b2):
        import jax, jax.numpy as jnp
        import numpy as np
        N_NODES = 3125
        N_EDGES = 100000
        NUM_REL = 8

        def _rgcn_layer(x, src, dst, edge_type, W, root, bias):
            out = x @ root + bias
            x_src = x[src]
            for r in range(W.shape[0]):
                mask = (edge_type == r).astype(x.dtype)
                s = jax.ops.segment_sum(x_src * mask[:, None], dst, num_segments=x.shape[0])
                cnt = jax.ops.segment_sum(mask, dst, num_segments=x.shape[0])
                agg = s / jnp.clip(cnt, 1.0)[:, None]
                out = out + agg @ W[r]
            return out
        src, dst = (edge_index[0], edge_index[1])
        h = _rgcn_layer(x, src, dst, edge_type, W1, root1, b1)
        h = jax.nn.relu(h)
        h = _rgcn_layer(h, src, dst, edge_type, W2, root2, b2)
        return h
    edge_index = jnp.stack([src, dst])
    x = _layernorm(x + _L0_gnn_ref(x, edge_attr_48, edge_attr_3, L0_gnn_fc0_w1, L0_gnn_fc0_b1, L0_gnn_fc0_w2, L0_gnn_fc0_b2, L0_gnn_fc1_w1, L0_gnn_fc1_b1, L0_gnn_fc1_w2, L0_gnn_fc1_b2, L0_gnn_bn0_gs, L0_gnn_bn0_bs, L0_gnn_bn0_gv, L0_gnn_bn1_gs, L0_gnn_bn1_bs, edge_index), axis=-1)
    x = _layernorm(x + _L1_gnn_ref(x, edge_index, edge_type_8, L1_gnn_W1, L1_gnn_root1, L1_gnn_b1, L1_gnn_W2, L1_gnn_root2, L1_gnn_b2), axis=-1)
    return x

_drawn_inputs = setup_inputs


def setup_inputs(seed=0):
    import zlib

    import numpy as np

    out = dict(_drawn_inputs(seed))
    spreads = {'L0_gnn_fc0_b1': (0.0, 0.1),
     'L0_gnn_fc0_b2': (0.0, 0.1),
     'L0_gnn_fc1_b1': (0.0, 0.1),
     'L0_gnn_fc1_b2': (0.0, 0.1),
     'L0_gnn_bn0_gs': (1.0, 0.2),
     'L0_gnn_bn0_bs': (0.0, 0.1),
     'L0_gnn_bn0_gv': (1.0, 0.2),
     'L0_gnn_bn1_gs': (1.0, 0.2),
     'L0_gnn_bn1_bs': (0.0, 0.1),
     'L1_gnn_b1': (0.0, 0.1),
     'L1_gnn_b2': (0.0, 0.36)}
    factors = {}
    for name, (base, spread) in spreads.items():
        noise = np.random.default_rng([zlib.crc32(name.encode()), seed]).standard_normal(out[name].shape)
        drawn = base * np.exp(spread * noise) if base else spread * noise
        out[name] = jnp.asarray(drawn.astype(out[name].dtype))
    for name, factor in factors.items():
        out[name] = (out[name] * factor).astype(out[name].dtype)
    return out
```

```python
import concourse.bass as bass
from concourse import mybir
from contextlib import ExitStack

NODES, EDGES = 3125, 103125
NS, NV, NREL, HID = 16, 4, 8, 32
FD = 3 * NS
EPS = 1e-5

P = 128
TILE_G = 4
GROUP = TILE_G * P
STEPS = -(-EDGES // (2 * GROUP))
GROUPS = 2 * STEPS
TILES = GROUPS * TILE_G
LO4, LO8, LO16 = 784, 392, 196
NPAD = 4 * LO4
CH = 98
C4, C8, C16 = LO4 // CH, LO8 // CH, LO16 // CH
NQ = NPAD // CH
F1 = NS + 3 * NV + 1
M1 = 4 * F1
FT = NS + 3 * NV + NREL
NW1 = (NS + NV) * NS
H1AT = 64
HROWS = FD + 1
PADS = NPAD - NODES
assert STEPS * 2 * GROUP >= EDGES and NODES < NPAD and PADS <= CH

K_IOTA, K_H29, K_H32, K_H16, K_END = 0, LO4, LO4 + M1, LO4 + M1 + P, LO4 + M1 + 2 * P
Q_ID, Q_CNT, Q_SUM, Q_SQ, Q_B0, Q_B1, Q_S16 = 0, P, P + M1, P + 2 * M1, P + 3 * M1, 2 * P + 3 * M1, 3 * P + 3 * M1
Q_PAD4 = 4 * P + 3 * M1
Q_ISS, Q_PAD8, Q_END = Q_PAD4 + 1, Q_PAD4 + 2, Q_PAD4 + 3


def gnn_kernel(nc, x, dst, src, typ, attr, vec, w1, fcb, w2a, w2b, bn0, bn1, rw1, rr1, rb1, rw2, rr2, rb2,
               cst16, cst32, out):
    f32, bf16, f16, i32 = mybir.dt.float32, mybir.dt.bfloat16, mybir.dt.float16, mybir.dt.int32
    ALU, ACT, AX = mybir.AluOpType, mybir.ActivationFunctionType, mybir.AxisListType.X
    ds = bass.ds

    hid_d = nc.dram_tensor("hid_d", (GROUPS, HROWS, GROUP), f32, kind="Internal").ap()
    row_d = nc.dram_tensor("row_d", (NPAD, FT), f32, kind="Internal").ap()
    cidx_d = nc.dram_tensor("cidx_d", (P, TILES), i32, kind="Internal").ap()
    y1_d = nc.dram_tensor("y1_d", (NPAD * NREL, HID), f32, kind="Internal").ap()
    y2_d = nc.dram_tensor("y2_d", (NPAD * NREL, NS), f32, kind="Internal").ap()

    ctx = ExitStack()
    with ctx:
        def sb(name, shape, dt=f32):
            return ctx.enter_context(nc.sbuf_tensor(name, shape, dt))

        def sem(name):
            return ctx.enter_context(nc.semaphore(name))

        def sems(name):
            return [sem(f"{name}{b}") for b in range(2)]

        k16, k32 = sb("k16", [P, K_END], f16), sb("k32", [P, Q_END])
        w1_s, fcb_s = sb("w1_s", [FD, H1AT + HROWS]), sb("fcb_s", [H1AT + HROWS, 1])
        w2a_s, w2b_s = sb("w2a_s", [HROWS, NW1]), sb("w2b_s", [HROWS, NW1])
        bn0_s, bn1_s = sb("bn0_s", [M1, 2]), sb("bn1_s", [P, 2])
        rb1_s, rb2_s = sb("rb1_s", [P, 1]), sb("rb2_s", [P, 1])
        rw1_s = sb("rw1_s", [P, 8, NREL * HID])
        rr1_s = sb("rr1_s", [P, 2, 4, HID])
        rw2_s = sb("rw2_s", [P, 4, NREL * NS])
        rr2_s = sb("rr2_s", [P, 2, 8, NS])
        src_i, dst_i, typ_i = sb("src_i", [P, TILES], i32), sb("dst_i", [P, TILES], i32), sb("typ_i", [P, TILES], i32)
        cidx_i = sb("cidx_i", [P, TILES], i32)
        typ_f = sb("typ_f", [P, TILES])
        s_hi4, s_lo4, s_hi8, s_lo8 = (sb(n, [P, TILES]) for n in ("s_hi4", "s_lo4", "s_hi8", "s_lo8"))
        d_hi4, d_lo4, d_hi8, d_lo8 = (sb(n, [P, TILES]) for n in ("d_hi4", "d_lo4", "d_hi8", "d_lo8"))
        d_lo16, d_seg, bit = sb("d_lo16", [P, TILES]), sb("d_seg", [P, TILES]), sb("bit", [P, TILES])
        vec_s, sh = sb("vec_s", [P, TILES, 3]), sb("sh", [P, TILES, 3])
        norm = sb("norm", [P, TILES])
        we = sb("we", [P, TILES])
        ix = [sb(f"ix{b}", [P, TILE_G], i32) for b in range(2)]
        attr_s = [sb(f"attr{b}", [FD, GROUP]) for b in range(2)]
        hid = [sb(f"hid{b}", [H1AT + HROWS, GROUP]) for b in range(2)]
        rows = [sb(f"rows{b}", [P, TILE_G * 40]) for b in range(2)]
        low = [sb(f"low{b}", [P, TILE_G, LO4], bf16) for b in range(2)]
        high = [sb(f"high{b}", [P, TILE_G * P], bf16) for b in range(2)]
        dlow = [sb(f"dlow{b}", [P, TILE_G, LO16], bf16) for b in range(2)]
        dseg = [sb(f"dseg{b}", [P, TILE_G, P], bf16) for b in range(2)]
        stk = [sb(f"stk{b}", [P, 3, TILE_G * P], bf16) for b in range(2)]
        prod = sb("prod", [P, 2, 2 * NW1])
        z = [sb(f"z{b}", [P, TILE_G, NS + NV]) for b in range(2)]
        msg = [sb(f"msg{b}", [P, TILE_G * HID]) for b in range(2)]
        part = sb("part", [P, 3, TILE_G * HID], bf16)
        rest = sb("rest", [P, TILE_G * HID])
        tmp4 = sb("tmp4", [P, TILE_G, NV])
        uvec = sb("uvec", [P, TILE_G, NV, 3])
        usum = sb("usum", [P, TILE_G, NV])
        tsel = sb("tsel", [P, TILE_G, NREL])
        tval = sb("tval", [P, TILE_G, NREL])
        acc = sb("acc", [P, LO4])
        rec = sb("rec", [P, LO4])
        sq = sb("sq", [P, LO4])
        cdt = sb("cdt", [P, LO16])
        st = sb("st", [P, 8])
        r2 = sb("r2", [CH, NQ, FT])
        xr = sb("xr", [CH, C8, 8 * NS])
        x1 = sb("x1", [CH, C8, 8 * NS])
        x2 = sb("x2", [CH, C8, 8 * NS])
        x1t = sb("x1t", [P, LO8])
        ht = sb("ht", [P, LO4])
        ysb = sb("ysb", [CH, C8 * 8 * NREL * HID])
        lnm, lnv, lnr = sb("lnm", [CH, NQ]), sb("lnv", [CH, NQ]), sb("lnr", [CH, NQ])
        lnd = sb("lnd", [CH, NQ, NS])

        PS = ctx.enter_context(nc.psum_tensor("PS", [P, 8, 512], f32))
        ACC, CNT, HP, WP = 0, 2, 3, 4

        s_small, s_edge, s_x = sem("small_loaded"), sem("edge_arrays_loaded"), sem("x_rows_loaded")
        s_blk, s_zero = sem("block_weights_loaded"), sem("cleared")
        s_ix = [sems(f"index_loaded{n}_") for n in range(4)]
        s_gat = [sems(f"rows_gathered{n}_") for n in range(4)]
        s_in = [sems(f"net_input_loaded{n}_") for n in range(2)]
        s_hid, s_relu, s_hst = sem("hidden_made"), sem("hidden_rectified"), sems("hidden_stored")
        s_w = [sem(f"weights_made{n}") for n in range(2)]
        s_prod = [sem(f"products_made{n}") for n in range(2)]
        s_red = [sem(f"messages_made{n}") for n in range(4)]
        s_cut = [sem(f"parts_cut{n}") for n in range(4)]
        s_mask = [sem(f"hi_onehot{n}") for n in range(4)]
        s_stk = [sem(f"stack_ready{n}") for n in range(4)]
        s_scat = [sem(f"group_summed{n}") for n in range(4)]
        s_z, s_u, s_t = sem("z_ready"), sem("u_ready"), sem("relation_weight")
        s_pre, s_sqrt, s_rt = sem("edge_arrays_made"), sem("norm_squared"), sem("norm_rooted")
        s_cidx, s_node, s_pe, s_act = sem("cidx_stored"), sem("node_step"), sem("node_product"), sem("node_root")
        s_tab, s_ysb, s_out = sem("table_stored"), sem("table_rows_made"), sem("out_stored")
        s_go = sem("gather_may_start")

        def k(col, n, rows_=P):
            return k32[0:rows_, col:col + n]

        def groups(eng, step):
            step(0, 0)
            step(1, 1)
            with eng.Fori(1, STEPS) as i:
                step(2 * i, 0)
                step(2 * i + 1, 1)

        def first(g):
            return isinstance(g, int) and g < 2

        def turn(g, b):
            return g // 2 + 1 if isinstance(g, int) else (g - b) // 2 + 1

        block = ctx.enter_context(nc.Block())

        @block.sync
        def _(eng):
            for t, s in ((k16, cst16), (k32, cst32), (w1_s, w1), (fcb_s, fcb), (w2a_s, w2a), (w2b_s, w2b),
                         (bn0_s, bn0), (bn1_s, bn1), (rb1_s, rb1), (rb2_s, rb2)):
                eng.dma_start(t[:, :], s).then_inc(s_small, 16)
            for t, s in ((src_i, src), (dst_i, dst), (typ_i, typ)):
                eng.dma_start(t[:, :], s).then_inc(s_edge, 16)
            eng.dma_start(vec_s[:, :, :], vec).then_inc(s_edge, 16)
            xv = x.rearrange("(h c p) f -> c p h f", c=C8, p=CH)
            for c in range(C8):
                eng.dma_start(xr[:, c, :].rearrange("p (h f) -> p h f", h=8), xv[c]).then_inc(s_x, 16)
            eng.wait_ge(s_zero, 1)
            for h in range(8):
                eng.dma_start(rw1_s[h * NS:(h + 1) * NS, h, :], rw1).then_inc(s_blk, 16)
                eng.dma_start(rr1_s[h * NS:(h + 1) * NS, h % 2, h // 2, :], rr1).then_inc(s_blk, 16)
                eng.dma_start(rr2_s[(h // 2) * HID:(h // 2 + 1) * HID, h % 2, h, :], rr2).then_inc(s_blk, 16)
            for h in range(4):
                eng.dma_start(rw2_s[h * HID:(h + 1) * HID, h, :], rw2).then_inc(s_blk, 16)

            def load_ix(n, g, b, idx):
                if not first(g):
                    eng.wait_ge(s_gat[n][b], (turn(g, b) - 1) * (16 * TILE_G))
                at = ds(g * TILE_G, TILE_G) if not isinstance(g, int) else slice(g * TILE_G, (g + 1) * TILE_G)
                eng.dma_start(ix[b][:, :], idx[:, at]).then_inc(s_ix[n][b], 16)

            def pass1(g, b):
                load_ix(0, g, b, dst)
                if not first(g):
                    eng.wait_ge(s_hid, g - 1)
                at = ds(g * GROUP, GROUP) if not isinstance(g, int) else slice(g * GROUP, (g + 1) * GROUP)
                eng.dma_start(attr_s[b][:, :], attr[:, at]).then_inc(s_in[0][b], 16)
            groups(eng, pass1)

            for b in range(2):
                eng.wait_ge(s_hst[b], 16 * STEPS)
                eng.wait_ge(s_gat[0][b], 16 * TILE_G * STEPS)

            def pass2(g, b):
                load_ix(1, g, b, dst)
                if not first(g):
                    eng.wait_ge(s_w[1], 2 * (g - 1))
                at = ds(g, 1) if not isinstance(g, int) else slice(g, g + 1)
                eng.dma_start(hid[b][0:HROWS, :], hid_d[at, :, :].rearrange("a k n -> k (a n)")).then_inc(s_in[1][b], 16)
            eng.wait_ge(s_w[0], 2 * GROUPS)
            groups(eng, pass2)

            eng.wait_ge(s_pre, 2)
            eng.dma_start(cidx_d, cidx_i[:, :]).then_inc(s_cidx, 16)
            eng.wait_ge(s_cidx, 16)
            for n in (2, 3):
                for b in range(2):
                    eng.wait_ge(s_gat[n - 1][b], 16 * TILE_G * STEPS)
                groups(eng, lambda g, b, n=n: load_ix(n, g, b, cidx_d))

            eng.wait_ge(s_node, NODE_OUT)
            ov = out.rearrange("(h c p) f -> c p h f", c=C8, p=CH)
            for c in range(C8):
                eng.dma_start(ov[c], x2[:, c, :].rearrange("p (h f) -> p h f", h=8)).then_inc(s_out, 16)
            eng.wait_ge(s_out, 16 * C8)

        @block.gpsimd
        def _(eng):
            for t in (rw1_s, rw2_s):
                eng.memset(t[:, :, :], 0.0)
            for t in (rr1_s, rr2_s):
                last = eng.memset(t[:, :, :, :], 0.0)
            last.then_inc(s_zero, 1)
            eng.wait_ge(s_zero, 1)

            def gather(n, g, b, table, width, used):
                eng.wait_ge(s_ix[n][b], 16 * turn(g, b))
                if not first(g):
                    used(g)
                eng.sem_inc(s_go, 1)
                for u in range(TILE_G):
                    eng.indirect_dma_start(rows[b][:, u * width:(u + 1) * width], None, table,
                                           bass.IndirectOffsetOnAxis(ix[b][:, u:u + 1], 0)).then_inc(s_gat[n][b], 16)

            groups(eng, lambda g, b: gather(0, g, b, x, NS, lambda g: eng.wait_ge(s_prod[0], 2 * (g - 1))))
            eng.wait_ge(s_prod[0], 2 * GROUPS)
            eng.wait_ge(s_tab, 16)

            def used2(g):
                eng.wait_ge(s_z, g - 1)
                eng.wait_ge(s_t, 3 * (g - 1))
                eng.wait_ge(s_u, 2 * (g - 1))
            groups(eng, lambda g, b: gather(1, g, b, row_d, FT, used2))
            used2(GROUPS + 1)
            eng.wait_ge(s_tab, 16 * (1 + C8))
            groups(eng, lambda g, b: gather(2, g, b, y1_d, HID, lambda g: eng.wait_ge(s_red[2], g - 1)))
            eng.wait_ge(s_red[2], GROUPS)
            eng.wait_ge(s_tab, 16 * (1 + C8 + C4))
            groups(eng, lambda g, b: gather(3, g, b, y2_d, NS, lambda g: eng.wait_ge(s_red[3], g - 1)))

        @block.tensor
        def _(eng):
            mm = nc.tensor.matmul
            eng.wait_ge(s_small, 160)
            eng.wait_ge(s_blk, 16 * 28)

            def scatter(n, g, b, cols, lo, halves):
                eng.wait_ge(s_stk[n], g + 1)
                for u in range(TILE_G):
                    for part_ in range(3):
                        for half in range(halves):
                            last = mm(PS[0:cols, ACC + half, 0:LO8], stk[b][:, part_, u * cols:(u + 1) * cols],
                                      low[b][:, u, half * LO8:(half + 1) * LO8], start=False, stop=True,
                                      skip_group_check=True)
                    if n == 0:
                        last = mm(PS[:, CNT, 0:LO16], dseg[b][:, u, :], dlow[b][:, u, :], start=False, stop=True,
                                  skip_group_check=True)
                last.then_inc(s_scat[n], 1)

            def make_hidden(g, b):
                eng.wait_ge(s_in[0][b], 16 * turn(g, b))
                if not (isinstance(g, int) and g == 0):
                    eng.wait_ge(s_relu, g)
                mm(PS[0:H1AT + HROWS, HP, :], w1_s[:, :], attr_s[b][:, :], start=True, stop=True).then_inc(s_hid, 1)

            def make_weights(n, g, w2, ready):
                b_ready, b = ready
                b_ready()
                for h in range(2):
                    if not (isinstance(g, int) and g == 0):
                        eng.wait_ge(s_prod[n], 2 * g - 1 + h)
                    for u in range(2):
                        last = mm(PS[:, WP + 2 * h + u, 0:NW1], hid[b][0:HROWS, (2 * h + u) * P:(2 * h + u + 1) * P],
                                  w2[:, :], start=True, stop=True)
                    last.then_inc(s_w[n], 1)

            def step1(g, b, more=True):
                make_weights(0, g, w2a_s, (lambda: eng.wait_ge(s_relu, g + 1), b))
                if more:
                    make_hidden(g + 1, 1 - b)
                if not (isinstance(g, int) and g == 0):
                    scatter(0, g - 1, 1 - b, M1, LO4, 2)

            eng.wait_ge(s_node, 1)
            for half in range(2):
                mm(PS[:, ACC + half, 0:LO8], sq[:, 0:P], sq[:, 0:LO8], start=True, stop=True, skip_group_check=True)
            mm(PS[:, CNT, 0:LO16], sq[:, 0:P], sq[:, 0:LO16], start=True, stop=True, skip_group_check=True)
            make_hidden(0, 0)
            step1(0, 0)
            step1(1, 1)
            with eng.Fori(1, STEPS - 1) as i:
                step1(2 * i, 0)
                step1(2 * i + 1, 1)
            step1(GROUPS - 2, 0)
            step1(GROUPS - 1, 1, more=False)
            scatter(0, GROUPS - 1, 1, M1, LO4, 2)

            pe = [0]

            def done(ins):
                pe[0] += 1
                ins.then_inc(s_pe, 1)

            eng.wait_ge(s_node, 3)
            for half in range(2):
                last = mm(PS[0:M1, HP + half, 0:LO8], k(Q_CNT, M1, M1), acc[0:M1, half * LO8:(half + 1) * LO8],
                          start=True, stop=True)
            done(last)
            eng.wait_ge(s_node, NODE_SUM1)
            done(mm(PS[0:M1, 5, 0:1], k(Q_SUM, M1, M1), st[0:M1, 0:1], start=True, stop=True))
            eng.wait_ge(s_node, NODE_SQ1)
            done(mm(PS[0:M1, 6, 0:1], k(Q_SQ, M1, M1), st[0:M1, 2:3], start=True, stop=True))
            for half in range(2):
                last = mm(PS[:, 7, 0:LO8], k(Q_B0 + half * P, P, M1), rec[0:M1, half * LO8:(half + 1) * LO8],
                          start=half == 0, stop=half == 1)
            done(last)
            eng.wait_ge(s_node, NODE_BN1)
            for c in range(C4):
                last = nc.tensor.transpose(PS[0:CH, c // 4, (c % 4) * M1:(c % 4 + 1) * M1],
                                           acc[0:M1, c * CH:(c + 1) * CH], k(Q_ID, M1, M1))
            for c in range(C16):
                last = nc.tensor.transpose(PS[0:CH, 2, c * P:(c + 1) * P], cdt[:, c * CH:(c + 1) * CH], k(Q_ID, P))
            done(last)

            eng.wait_ge(s_node, NODE_ROWS1)
            mm(PS[:, ACC, 0:LO8], sq[:, 0:P], sq[:, 0:LO8], start=True, stop=True, skip_group_check=True)

            def step2(g, b):
                make_weights(1, g, w2b_s, (lambda: eng.wait_ge(s_in[1][b], 16 * turn(g, b)), b))
                if not (isinstance(g, int) and g == 0):
                    scatter(1, g - 1, 1 - b, P, LO8, 1)
            groups(eng, step2)
            scatter(1, GROUPS - 1, 1, P, LO8, 1)

            eng.wait_ge(s_node, NODE_SUM2)
            done(mm(PS[:, 5, 0:1], k(Q_S16, P), st[:, 0:1], start=True, stop=True))
            eng.wait_ge(s_node, NODE_SQ2)
            done(mm(PS[:, 6, 0:1], k(Q_S16, P), st[:, 2:3], start=True, stop=True))
            eng.wait_ge(s_node, NODE_BN2)
            for c in range(C8):
                last = nc.tensor.transpose(PS[0:CH, 2, c * P:(c + 1) * P], acc[:, c * CH:(c + 1) * CH], k(Q_ID, P))
            done(last)
            eng.wait_ge(s_node, NODE_X1)
            for c in range(C8):
                last = nc.tensor.transpose(PS[:, 3, c * CH:(c + 1) * CH], x1[:, c, :], k(Q_ID, CH, CH))
            done(last)
            eng.wait_ge(s_node, NODE_X1T)
            for half in range(2):
                mm(PS[:, ACC + half, 0:LO8], rr1_s[:, half, :, :].rearrange("p h f -> p (h f)"), x1t[:, :],
                   start=True, stop=True, skip_group_check=True)
            for n in range(4 * C8):
                if n >= 2:
                    eng.wait_ge(s_ysb, n - 1)
                done(mm(PS[0:CH, 4 + n % 2, :], x1t[:, (n // 4) * CH:(n // 4 + 1) * CH],
                        rw1_s[:, 2 * (n % 4):2 * (n % 4) + 2, :].rearrange("p h r -> p (h r)"), start=True, stop=True))
            groups(eng, lambda g, b: scatter(2, g, b, P, LO4, 2))

            eng.wait_ge(s_act, ACT_H)
            for half in range(2):
                mm(PS[:, 2, 0:LO8], rr2_s[:, half, :, :].rearrange("p h f -> p (h f)"),
                   ht[:, half * LO8:(half + 1) * LO8], start=half == 0, stop=half == 1, skip_group_check=True)
            for n in range(C4):
                eng.wait_ge(s_ysb, 4 * C8 + n - 1)
                done(mm(PS[0:CH, 4 + n % 2, :], ht[:, n * CH:(n + 1) * CH], rw2_s[:, :, :].rearrange("p h r -> p (h r)"),
                        start=True, stop=True))

            def scatter4(g, b):
                eng.wait_ge(s_stk[3], g + 1)
                for u in range(TILE_G):
                    for part_ in range(3):
                        last = mm(PS[:, 2, 0:LO8], stk[b][:, part_, u * P:(u + 1) * P], low[b][:, u, 0:LO8],
                                  start=False, stop=True, skip_group_check=True)
                last.then_inc(s_scat[3], 1)
            groups(eng, scatter4)
            eng.wait_ge(s_node, NODE_B2)
            for c in range(C8):
                last = nc.tensor.transpose(PS[0:CH, 3, c * P:(c + 1) * P], acc[:, c * CH:(c + 1) * CH], k(Q_ID, P))
            done(last)
            assert pe[0] == PE_OUT

        @block.scalar
        def _(eng):
            act = nc.scalar.activation
            eng.wait_ge(s_sqrt, 1)
            act(norm[:, :], norm[:, :], ACT.Sqrt).then_inc(s_rt, 1)
            eng.wait_ge(s_small, 160)

            def rectify(g, b):
                eng.wait_ge(s_hid, g + 1)
                if not first(g):
                    eng.wait_ge(s_w[0], 2 * (g - 1))
                    eng.wait_ge(s_hst[b], 16 * (turn(g, b) - 1))
                act(hid[b][:, :], PS[0:H1AT + HROWS, HP, :], ACT.Relu, bias=fcb_s[:, 0:1]).then_inc(s_relu, 1)
                eng.wait_ge(s_relu, g + 1)
                at = ds(g, 1) if not isinstance(g, int) else slice(g, g + 1)
                eng.dma_start(hid_d[at, :, :].rearrange("a k n -> k (a n)"), hid[b][H1AT:H1AT + HROWS, :])\
                   .then_inc(s_hst[b], 16)
            groups(eng, rectify)

            def root(n, value):
                eng.wait_ge(s_node, value)
                act(st[0:n, 3:4], st[0:n, 3:4], ACT.Sqrt).then_inc(s_act, 1)
            root(M1, NODE_VAR1)
            eng.wait_ge(s_node, NODE_ROWS1)
            eng.dma_start(row_d.rearrange("(q p) f -> p q f", p=CH), r2[:, :, :]).then_inc(s_tab, 16)

            def inputs2(g, b):
                eng.wait_ge(s_gat[1][b], 16 * TILE_G * turn(g, b))
                if not first(g):
                    eng.wait_ge(s_prod[1], 2 * (g - 1))
                rv = rows[b][:, 0:TILE_G * FT].rearrange("p (t f) -> p t f", f=FT)
                act(z[b][:, :, 0:NS], rv[:, :, 0:NS], ACT.Copy).then_inc(s_z, 1)
            groups(eng, inputs2)
            root(P, NODE_VAR2)
            eng.wait_ge(s_node, NODE_LN1)
            act(lnr[:, :], lnv[:, :], ACT.Sqrt).then_inc(s_act, 1)
            y1v = ysb[:, :].rearrange("p (c n) -> p c n", c=4 * C8)
            yd = y1_d.rearrange("(h c p r) f -> c p h (r f)", h=8, c=C8, p=CH)
            for c in range(C8):
                eng.wait_ge(s_ysb, 4 * (c + 1))
                eng.dma_start(yd[c], ysb[:, c * 8 * NREL * HID:(c + 1) * 8 * NREL * HID]
                              .rearrange("p (h r) -> p h r", h=8)).then_inc(s_tab, 16)
            eng.wait_ge(s_scat[2], GROUPS)
            for half in range(2):
                last = act(ht[:, half * LO8:(half + 1) * LO8], PS[:, ACC + half, 0:LO8], ACT.Relu, bias=rb1_s[:, 0:1])
            last.then_inc(s_act, 1)
            yd = y2_d.rearrange("(h c p r) f -> c p h (r f)", h=4, c=C4, p=CH)
            for c in range(C4):
                eng.wait_ge(s_ysb, 4 * C8 + c + 1)
                eng.dma_start(yd[c], ysb[:, c * 512:(c + 1) * 512].rearrange("p (h r) -> p h r", h=4))\
                   .then_inc(s_tab, 16)
            eng.wait_ge(s_node, NODE_LN2)
            act(lnr[:, :], lnv[:, :], ACT.Sqrt).then_inc(s_act, 1)
            eng.wait_ge(s_tab, 16 * (1 + C8 + C4))

        @block.vector
        def _(eng):
            v = nc.vector
            node = [0]

            def link(ins):
                node[0] += 1
                ins.then_inc(s_node, 1)
                eng.wait_ge(s_node, node[0])

            def at(name, value):
                assert node[0] == value, (name, node[0])

            link(v.memset(sq[:, :], 0.0))
            for b in range(2):
                last = v.memset(msg[b][:, :], 1.0)
            link(last)
            eng.wait_ge(s_edge, 64)
            chain = [0]

            def step(ins):
                chain[0] += 1
                ins.then_inc(s_sqrt, 1)
                eng.wait_ge(s_sqrt, chain[0])

            vf = vec_s[:, :, :].rearrange("p t c -> p (t c)")
            shf = sh[:, :, :].rearrange("p t c -> p (t c)")
            v.tensor_tensor(shf, vf, vf, ALU.mult).then_inc(s_rt, 1)
            eng.wait_ge(s_rt, 1)
            v.tensor_reduce(norm[:, :], sh[:, :, :], AX, ALU.add).then_inc(s_sqrt, 1)
            chain[0] += 1
            step(v.tensor_copy(typ_f[:, :], typ_i[:, :]))

            def split(i, hi4, lo4, hi8, lo8):
                step(v.tensor_copy(lo4[:, :], i[:, :]))
                step(v.tensor_scalar(hi4[:, :], lo4[:, :], float(LO4), None, ALU.is_ge))
                for m in (2, 3):
                    step(v.scalar_tensor_tensor(hi4[:, :], lo4[:, :], float(m * LO4), hi4[:, :], ALU.is_ge, ALU.add))
                step(v.scalar_tensor_tensor(lo4[:, :], hi4[:, :], -float(LO4), lo4[:, :], ALU.mult, ALU.add))
                step(v.tensor_scalar(bit[:, :], lo4[:, :], float(LO8), None, ALU.is_ge))
                step(v.scalar_tensor_tensor(hi8[:, :], hi4[:, :], 2.0, bit[:, :], ALU.mult, ALU.add))
                step(v.scalar_tensor_tensor(lo8[:, :], bit[:, :], -float(LO8), lo4[:, :], ALU.mult, ALU.add))
            step(v.tensor_copy(we[:, :], src_i[:, :]))
            step(v.scalar_tensor_tensor(we[:, :], we[:, :], float(NREL), typ_f[:, :], ALU.mult, ALU.add))
            v.tensor_copy(cidx_i[:, :], we[:, :]).then_inc(s_pre, 2)
            split(src_i, s_hi4, s_lo4, s_hi8, s_lo8)
            split(dst_i, d_hi4, d_lo4, d_hi8, d_lo8)
            step(v.tensor_scalar(bit[:, :], d_lo8[:, :], float(LO16), None, ALU.is_ge))
            step(v.scalar_tensor_tensor(d_lo16[:, :], bit[:, :], -float(LO16), d_lo8[:, :], ALU.mult, ALU.add))
            step(v.scalar_tensor_tensor(d_seg[:, :], d_hi8[:, :], 2.0, bit[:, :], ALU.mult, ALU.add))
            step(v.scalar_tensor_tensor(d_seg[:, :], d_seg[:, :], float(NREL), typ_f[:, :], ALU.mult, ALU.add))
            eng.wait_ge(s_rt, 2)
            step(v.tensor_scalar(norm[:, :], norm[:, :], 1e-12, None, ALU.add))
            step(v.reciprocal(norm[:, :], norm[:, :]))
            step(v.tensor_tensor(sh[:, :, :], vec_s[:, :, :], norm[:, :].unsqueeze(2).broadcast_to([P, TILES, 3]), ALU.mult))
            step(v.tensor_scalar(shf, shf, 3.0 ** 0.5, None, ALU.mult))

            eng.wait_ge(s_small, 160)
            eng.wait_ge(s_pre, 2)

            def tile(g, u):
                return ds(g * TILE_G + u, 1) if not isinstance(g, int) else slice(g * TILE_G + u, g * TILE_G + u + 1)

            def tiles(g):
                return ds(g * TILE_G, TILE_G) if not isinstance(g, int) else slice(g * TILE_G, (g + 1) * TILE_G)

            def onehots(n, g, b, cols, kcol, hi, lo, width):
                if not first(g):
                    eng.wait_ge(s_scat[n], g - 1)
                for u in range(TILE_G):
                    v.tensor_scalar(low[b][:, u, 0:width], k16[:, K_IOTA:K_IOTA + width], lo[:, tile(g, u)], None,
                                    ALU.is_equal)
                    if n == 0:
                        v.tensor_scalar(dlow[b][:, u, :], k16[:, K_IOTA:K_IOTA + LO16], d_lo16[:, tile(g, u)], None,
                                        ALU.is_equal)
                        v.tensor_scalar(dseg[b][:, u, :], k16[:, K_IOTA:K_IOTA + P], d_seg[:, tile(g, u)], None,
                                        ALU.is_equal)
                    last = v.tensor_scalar(high[b][:, u * cols:(u + 1) * cols], k16[:, kcol:kcol + cols],
                                           hi[:, tile(g, u)], None, ALU.is_equal)
                last.then_inc(s_mask[n], 1)

            def stack(n, g, b, a, f):
                w = TILE_G * f
                eng.wait_ge(s_red[n], (g + 1) * (5 if n == 0 else 2 if n == 1 else 1))
                v.tensor_copy(part[:, 0, 0:w], msg[b][:, 0:w]).then_inc(s_cut[n], 1)
                eng.wait_ge(s_cut[n], 4 * g + 1)
                v.tensor_tensor(rest[:, 0:w], msg[b][:, 0:w], part[:, 0, 0:w], ALU.subtract).then_inc(s_cut[n], 1)
                eng.wait_ge(s_cut[n], 4 * g + 2)
                v.tensor_copy(part[:, 1, 0:w], rest[:, 0:w]).then_inc(s_cut[n], 1)
                eng.wait_ge(s_cut[n], 4 * g + 3)
                v.tensor_tensor(part[:, 2, 0:w], rest[:, 0:w], part[:, 1, 0:w], ALU.subtract).then_inc(s_cut[n], 1)
                eng.wait_ge(s_mask[n], g + 1)
                eng.wait_ge(s_cut[n], 4 * g + 4)
                for m in range(3):
                    last = v.tensor_tensor(
                        stk[b][:, m, 0:w * a].rearrange("p (t h f) -> p t h f", h=a, f=f),
                        high[b][:, 0:w * a].rearrange("p (t h f) -> p t h f", h=a, f=f),
                        part[:, m, 0:w].rearrange("p (t f) -> p t f", f=f).unsqueeze(2).broadcast_to([P, TILE_G, a, f]),
                        ALU.mult)
                last.then_inc(s_stk[n], 1)

            def products(n, g, h, x_in, nj, ni):
                eng.wait_ge(s_w[n], 2 * g + 1 + h)
                v.tensor_tensor(prod[:, h, :].rearrange("p (t j i) -> p t j i", t=2, j=nj),
                                PS[:, WP + 2 * h:WP + 2 * h + 2, 0:NW1].rearrange("p t (j i) -> p t j i", j=nj),
                                x_in[:, 2 * h:2 * h + 2, :].unsqueeze(2).broadcast_to([P, 2, nj, ni]),
                                ALU.mult).then_inc(s_prod[n], 1)

            def pass1(g, b):
                onehots(0, g, b, M1, K_H29, s_hi4, s_lo4, LO4)
                eng.wait_ge(s_gat[0][b], 16 * TILE_G * turn(g, b))
                xg = rows[b][:, 0:TILE_G * NS].rearrange("p (t f) -> p t f", f=NS)
                mv = msg[b][:, 0:TILE_G * F1].rearrange("p (t f) -> p t f", f=F1)
                for h in range(2):
                    products(0, g, h, xg, NS + NV, NS)
                for h in range(2):
                    eng.wait_ge(s_prod[0], 2 * g + 1 + h)
                    pv = prod[:, h, :].rearrange("p (t j i) -> p t j i", t=2, j=NS + NV)
                    v.tensor_reduce(mv[:, 2 * h:2 * h + 2, 0:NS], pv[:, :, 0:NS, :], AX, ALU.add).then_inc(s_red[0], 1)
                    v.tensor_reduce(tmp4[:, 2 * h:2 * h + 2, :], pv[:, :, NS:NS + NV, :], AX, ALU.add).then_inc(s_red[0], 1)
                eng.wait_ge(s_red[0], 5 * g + 4)
                v.tensor_tensor(mv[:, :, NS:NS + 3 * NV].rearrange("p t (j c) -> p t j c", c=3),
                                tmp4[:, :, :].unsqueeze(3).broadcast_to([P, TILE_G, NV, 3]),
                                sh[:, tiles(g), :].unsqueeze(2).broadcast_to([P, TILE_G, NV, 3]),
                                ALU.mult).then_inc(s_red[0], 1)
                stack(0, g, b, 4, F1)
            groups(eng, pass1)

            at("start", 2)
            eng.wait_ge(s_scat[0], GROUPS)
            link(v.tensor_copy(acc[0:M1, :].rearrange("p (a n) -> p a n", a=2), PS[0:M1, ACC:ACC + 2, 0:LO8]))
            link(v.tensor_scalar(cdt[:, :], PS[:, CNT, 0:LO16], 1.0, None, ALU.max))
            link(v.reciprocal(cdt[:, :], cdt[:, :]))
            eng.wait_ge(s_pe, 1)
            link(v.tensor_scalar(rec[0:M1, :].rearrange("p (a n) -> p a n", a=2), PS[0:M1, HP:HP + 2, 0:LO8], 1.0, None,
                                 ALU.max))
            link(v.reciprocal(rec[0:M1, :], rec[0:M1, :]))
            link(v.scalar_tensor_tensor(acc[0:M1, :], acc[0:M1, :], NS ** -0.5, rec[0:M1, :], ALU.mult, ALU.mult))

            def batch_norm(n, width, bank_sum, pe_sum, pad_col, only, bn, n_act):
                def clear_pads():
                    link(v.tensor_scalar(acc[0:n, width - PADS:width], acc[0:n, width - PADS:width],
                                         k(pad_col, 1, n), None, ALU.mult))
                clear_pads()
                link(v.tensor_reduce(st[0:n, 0:1], acc[0:n, 0:width], AX, ALU.add))
                yield
                eng.wait_ge(s_pe, pe_sum)
                if only is None:
                    link(v.tensor_scalar(st[0:n, 1:2], PS[0:n, 5, 0:1], 1.0 / NODES, None, ALU.mult))
                else:
                    link(v.tensor_scalar(st[0:n, 1:2], PS[0:n, 5, 0:1], k(only, 1, n), 1.0 / NODES, ALU.mult, ALU.mult))
                link(v.tensor_scalar(acc[0:n, 0:width], acc[0:n, 0:width], st[0:n, 1:2], None, ALU.subtract))
                clear_pads()
                link(v.tensor_tensor(sq[0:n, 0:width], acc[0:n, 0:width], acc[0:n, 0:width], ALU.mult))
                link(v.tensor_reduce(st[0:n, 2:3], sq[0:n, 0:width], AX, ALU.add))
                yield
                eng.wait_ge(s_pe, pe_sum + 1)
                link(v.tensor_scalar(st[0:n, 3:4], PS[0:n, 6, 0:1], 1.0 / NODES, EPS, ALU.mult, ALU.add))
                yield
                eng.wait_ge(s_act, n_act)
                link(v.reciprocal(st[0:n, 4:5], st[0:n, 3:4]))
                link(v.tensor_tensor(st[0:n, 4:5], st[0:n, 4:5], bn[0:n, 0:1], ALU.mult))
                link(v.tensor_scalar(acc[0:n, 0:width], acc[0:n, 0:width], st[0:n, 4:5], bn[0:n, 1:2], ALU.mult, ALU.add))
                yield
            stage = batch_norm(M1, LO4, 5, 2, Q_PAD4, Q_ISS, bn0_s, 1)
            for name, value in (("sum", NODE_SUM1), ("sq", NODE_SQ1), ("var", NODE_VAR1), ("bn", NODE_BN1)):
                next(stage)
                at(name, value)
            eng.wait_ge(s_pe, 5)
            r2v = r2[:, :, 0:FT - NREL].rearrange("p (h c) f -> p c h f", h=4)
            for c in range(C4):
                link(v.tensor_copy(r2v[:, c], PS[0:CH, c // 4, (c % 4) * M1:(c % 4 + 1) * M1]
                                   .rearrange("p (h f) -> p h f", h=4)[:, :, 0:F1 - 1]))
            r2c = r2[:, :, FT - NREL:FT].rearrange("p (h c) f -> p c h f", h=16)
            for c in range(C16):
                link(v.tensor_copy(r2c[:, c], PS[0:CH, 2, c * P:(c + 1) * P].rearrange("p (h f) -> p h f", h=16)))
            link(v.tensor_copy(rec[:, 0:LO8], PS[:, 7, 0:LO8]))
            link(v.memset(sq[:, :], 0.0))
            at("rows1", NODE_ROWS1)

            def pass2(g, b):
                onehots(1, g, b, P, K_H16, s_hi8, s_lo8, LO8)
                eng.wait_ge(s_gat[1][b], 16 * TILE_G * turn(g, b))
                rv = rows[b][:, 0:TILE_G * FT].rearrange("p (t f) -> p t f", f=FT)
                v.tensor_tensor(uvec[:, :, :, :], rv[:, :, NS:NS + 3 * NV].rearrange("p t (j c) -> p t j c", c=3),
                                sh[:, tiles(g), :].unsqueeze(2).broadcast_to([P, TILE_G, NV, 3]), ALU.mult).then_inc(s_u, 1)
                v.tensor_tensor(tsel[:, :, :], k16[:, K_IOTA:K_IOTA + NREL].unsqueeze(1).broadcast_to([P, TILE_G, NREL]),
                                typ_f[:, tiles(g)].unsqueeze(2).broadcast_to([P, TILE_G, NREL]), ALU.is_equal)\
                 .then_inc(s_t, 1)
                eng.wait_ge(s_u, 2 * g + 1)
                v.tensor_reduce(usum[:, :, :], uvec[:, :, :, :], AX, ALU.add).then_inc(s_u, 1)
                eng.wait_ge(s_t, 3 * g + 1)
                v.tensor_tensor(tval[:, :, :], tsel[:, :, :], rv[:, :, FT - NREL:FT], ALU.mult).then_inc(s_t, 1)
                eng.wait_ge(s_u, 2 * g + 2)
                v.tensor_scalar(z[b][:, :, NS:NS + NV], usum[:, :, :], 3.0 ** -0.5, None, ALU.mult).then_inc(s_red[1], 1)
                eng.wait_ge(s_t, 3 * g + 2)
                v.tensor_reduce(we[:, tiles(g)], tval[:, :, :], AX, ALU.add).then_inc(s_t, 1)
                eng.wait_ge(s_red[1], 2 * g + 1)
                eng.wait_ge(s_z, g + 1)
                mv = msg[b][:, 0:TILE_G * NS].rearrange("p (t f) -> p t f", f=NS)
                for h in range(2):
                    products(1, g, h, z[b], NS, NS + NV)
                for h in range(2):
                    eng.wait_ge(s_prod[1], 2 * g + 1 + h)
                    pv = prod[:, h, :].rearrange("p (t j i) -> p t j i", t=2, j=NS)
                    last = v.tensor_reduce(mv[:, 2 * h:2 * h + 2, :], pv, AX, ALU.add)
                last.then_inc(s_red[1], 1)
                stack(1, g, b, 8, NS)
            groups(eng, pass2)

            eng.wait_ge(s_scat[1], GROUPS)
            link(v.scalar_tensor_tensor(acc[:, 0:LO8], PS[:, ACC, 0:LO8], (NS + NV) ** -0.5, rec[:, 0:LO8],
                                        ALU.mult, ALU.mult))
            stage = batch_norm(P, LO8, 5, 6, Q_PAD8, None, bn1_s, 2)
            for name, value in (("sum", NODE_SUM2), ("sq", NODE_SQ2), ("var", NODE_VAR2), ("bn", NODE_BN2)):
                next(stage)
                at(name, value)

            def layer_norm(bank, plus, to, n_act):
                d = lnd[:, :, :].rearrange("p q f -> p (q f)")
                link(v.tensor_tensor(to[:, :, :].rearrange("p c n -> p (c n)"), PS[0:CH, bank, :],
                                     plus[:, :, :].rearrange("p c n -> p (c n)"), ALU.add))
                tv = to[:, :, :].rearrange("p c (h f) -> p (c h) f", f=NS)
                wide = [CH, NQ, NS]
                link(v.tensor_reduce(lnm[:, :], tv, AX, ALU.add))
                link(v.tensor_scalar(lnm[:, :], lnm[:, :], 1.0 / NS, None, ALU.mult))
                link(v.tensor_tensor(tv, tv, lnm[:, :].unsqueeze(2).broadcast_to(wide), ALU.subtract))
                link(v.tensor_tensor(lnd[:, :, :], tv, tv, ALU.mult))
                link(v.tensor_reduce(lnv[:, :], lnd[:, :, :], AX, ALU.add))
                link(v.tensor_scalar(lnv[:, :], lnv[:, :], 1.0 / NS, EPS, ALU.mult, ALU.add))
                yield
                eng.wait_ge(s_act, n_act)
                link(v.reciprocal(lnr[:, :], lnr[:, :]))
                link(v.tensor_tensor(tv, tv, lnr[:, :].unsqueeze(2).broadcast_to(wide), ALU.mult))
                yield
            eng.wait_ge(s_pe, 8)
            eng.wait_ge(s_x, 16 * C8)
            stage = layer_norm(2, xr, x1, 3)
            next(stage)
            at("ln1", NODE_LN1)
            next(stage)
            at("x1", NODE_X1)
            eng.wait_ge(s_pe, 9)
            link(v.tensor_copy(x1t[:, :], PS[:, 3, 0:LO8]))
            at("x1t", NODE_X1T)
            y1v = ysb[:, :].rearrange("p (n m) -> p n m", m=512)
            for n in range(4 * C8):
                eng.wait_ge(s_pe, 10 + n)
                v.tensor_copy(y1v[:, n, :], PS[0:CH, 4 + n % 2, :]).then_inc(s_ysb, 1)

            def relational(n, g, b, a, f, kcol, hi, lo, width):
                onehots(n, g, b, P, kcol, hi, lo, width)
                eng.wait_ge(s_gat[n][b], 16 * TILE_G * turn(g, b))
                v.tensor_tensor(msg[b][:, 0:TILE_G * f].rearrange("p (t f) -> p t f", f=f),
                                rows[b][:, 0:TILE_G * f].rearrange("p (t f) -> p t f", f=f),
                                we[:, tiles(g)].unsqueeze(2).broadcast_to([P, TILE_G, f]), ALU.mult).then_inc(s_red[n], 1)
                stack(n, g, b, a, f)
            groups(eng, lambda g, b: relational(2, g, b, 4, HID, K_H32, d_hi4, d_lo4, LO4))
            eng.wait_ge(s_tab, 16 * (1 + C8))
            for n in range(C4):
                eng.wait_ge(s_pe, 10 + 4 * C8 + n)
                v.tensor_copy(y1v[:, n, :], PS[0:CH, 4 + n % 2, :]).then_inc(s_ysb, 1)
            groups(eng, lambda g, b: relational(3, g, b, 8, NS, K_H16, d_hi8, d_lo8, LO8))
            eng.wait_ge(s_scat[3], GROUPS)
            link(v.tensor_scalar(acc[:, 0:LO8], PS[:, 2, 0:LO8], rb2_s[:, 0:1], None, ALU.add))
            at("b2", NODE_B2)
            eng.wait_ge(s_pe, PE_OUT)
            stage = layer_norm(3, x1, x2, 5)
            next(stage)
            at("ln2", NODE_LN2)
            next(stage)
            at("out", NODE_OUT)


NODE_SUM1 = 10
NODE_SQ1 = NODE_SUM1 + 5
NODE_VAR1 = NODE_SQ1 + 1
NODE_BN1 = NODE_VAR1 + 3
NODE_ROWS1 = NODE_BN1 + C4 + C16 + 2
NODE_SUM2 = NODE_ROWS1 + 3
NODE_SQ2 = NODE_SUM2 + 5
NODE_VAR2 = NODE_SQ2 + 1
NODE_BN2 = NODE_VAR2 + 3
NODE_LN1 = NODE_BN2 + 7
NODE_X1 = NODE_LN1 + 2
NODE_X1T = NODE_X1 + 1
NODE_B2 = NODE_X1T + 1
NODE_LN2 = NODE_B2 + 7
NODE_OUT = NODE_LN2 + 2
ACT_H = 4
PE_OUT = 9 + 4 * C8 + C4 + 1


def _constants(np):
    row = np.concatenate([np.arange(LO4), np.repeat(np.arange(4), F1), np.repeat(np.arange(4), HID),
                          np.repeat(np.arange(8), NS)])
    c16 = np.ascontiguousarray(np.broadcast_to(row.astype(np.float16), (P, K_END)))
    c32 = np.zeros((P, Q_END), np.float32)
    q, m = np.arange(M1)[:, None], np.arange(M1)[None, :]
    qf, mf = q % F1, m % F1
    c32[:, Q_ID:Q_ID + P] = np.eye(P)
    c32[:M1, Q_CNT:Q_CNT + M1] = (qf == F1 - 1) & (q // F1 == m // F1)
    c32[:M1, Q_SUM:Q_SUM + M1] = qf == mf
    both = (qf >= NS) & (mf >= NS) & (qf < F1 - 1) & (mf < F1 - 1) & ((qf - NS) // 3 == (mf - NS) // 3)
    c32[:M1, Q_SQ:Q_SQ + M1] = np.where(qf < NS, qf == mf, both / 3)
    wide = np.arange(P)[None, :]
    for b in range(2):
        c32[:M1, Q_B0 + b * P:Q_B0 + (b + 1) * P] = (qf == F1 - 1) & (wide // NS == 2 * (q // F1) + b)
    c32[:, Q_S16:Q_S16 + P] = np.arange(P)[:, None] % NS == wide % NS
    c32[:M1, Q_PAD4] = np.arange(M1) // F1 < 3
    c32[:M1, Q_ISS] = np.arange(M1) % F1 < NS
    c32[:, Q_PAD8] = np.arange(P) // NS < 7
    return c16, c32


def kernel(**inputs):
    import numpy as np
    import concourse.bacc as bacc
    from concourse.bass_utils import run_bass_kernel_spmd

    a = {n: np.asarray(v) for n, v in inputs.items()}
    slots = TILES * P

    def edges(v, fill):
        full = np.full((slots,) + v.shape[1:], fill, v.dtype)
        full[:EDGES] = v
        return np.ascontiguousarray(full.reshape((TILES, P) + v.shape[1:]).swapaxes(0, 1))

    x = np.zeros((NPAD, NS), np.float32)
    x[:NODES] = a["x"]
    attr = np.zeros((FD, slots), np.float32)
    attr[:, :EDGES] = a["edge_attr_48"].T
    w1 = np.zeros((FD, H1AT + HROWS), np.float32)
    fcb = np.zeros((H1AT + HROWS, 1), np.float32)
    for n, at in ((0, 0), (1, H1AT)):
        w1[:, at:at + FD] = a[f"L0_gnn_fc{n}_w1"]
        fcb[at:at + FD, 0] = a[f"L0_gnn_fc{n}_b1"]
        fcb[at + FD, 0] = 1

    def weights(n):
        w = np.concatenate([a[f"L0_gnn_fc{n}_w2"], a[f"L0_gnn_fc{n}_b2"][None]])
        s, v = w[:, :NS * NS].reshape(HROWS, NS, NS), w[:, NS * NS:]
        if n == 0:
            w = np.concatenate([s, v.reshape(HROWS, NS, NV)], 2)
        else:
            w = np.concatenate([s, v.reshape(HROWS, NV, NS)], 1)
        return np.ascontiguousarray(w.transpose(0, 2, 1).reshape(HROWS, NW1))

    bn0 = np.zeros((4, F1, 2), np.float32)
    bn0[:, :NS, 0], bn0[:, :NS, 1] = a["L0_gnn_bn0_gs"], a["L0_gnn_bn0_bs"]
    bn0[:, NS:F1 - 1, 0] = np.repeat(a["L0_gnn_bn0_gv"], 3)
    bn1 = np.tile(np.stack([a["L0_gnn_bn1_gs"], a["L0_gnn_bn1_bs"]], 1), (8, 1))
    c16, c32 = _constants(np)
    arrays = {
        "x": x, "dst": edges(a["dst"], NODES), "src": edges(a["src"], NODES), "typ": edges(a["edge_type_8"], 0),
        "attr": attr, "vec": edges(a["edge_attr_3"], 0), "w1": w1, "fcb": fcb, "w2a": weights(0), "w2b": weights(1),
        "bn0": bn0.reshape(M1, 2), "bn1": bn1,
        "rw1": np.ascontiguousarray(a["L1_gnn_W1"].transpose(1, 0, 2).reshape(NS, NREL * HID)),
        "rr1": a["L1_gnn_root1"], "rb1": np.tile(a["L1_gnn_b1"], 4)[:, None],
        "rw2": np.ascontiguousarray(a["L1_gnn_W2"].transpose(1, 0, 2).reshape(HID, NREL * NS)),
        "rr2": a["L1_gnn_root2"], "rb2": np.tile(a["L1_gnn_b2"], 8)[:, None], "cst16": c16, "cst32": c32,
    }
    nc = bacc.Bacc("TRN2", target_bir_lowering=False, num_devices=1)
    arrays = {f"in_{n}": np.ascontiguousarray(v) for n, v in arrays.items()}
    args = [nc.dram_tensor(n, v.shape, mybir.dt.from_np(v.dtype), kind="ExternalInput").ap() for n, v in arrays.items()]
    out = nc.dram_tensor("out", (NPAD, NS), mybir.dt.float32, kind="ExternalOutput").ap()
    gnn_kernel(nc, *args, out)
    r = run_bass_kernel_spmd(nc, [arrays], core_ids=[0])
    return np.ascontiguousarray(r.results[0]["out"][:NODES])
```

```python
import concourse.bass as bass
from concourse import mybir
from contextlib import ExitStack

NODES, EDGES = 3125, 103125
NS, NV, NREL, HID = 16, 4, 8, 32
FD = 3 * NS
EPS = 1e-5

P = 128
TILE_G = 4
GROUP = TILE_G * P
STEPS = -(-EDGES // (2 * GROUP))
GROUPS = 2 * STEPS
TILES = GROUPS * TILE_G
LO4, LO8, LO16 = 784, 392, 196
NPAD = 4 * LO4
CH = 98
C4, C8, C16 = LO4 // CH, LO8 // CH, LO16 // CH
NQ = NPAD // CH
Y1_EACH = 2 * C8
F1 = NS + 3 * NV + 1
M1 = 4 * F1
FT = NS + 3 * NV + NREL
NW1 = (NS + NV) * NS
H1AT = 64
HROWS = FD + 1
PADS = NPAD - NODES
LOW_ACT = 3
assert STEPS * 2 * GROUP >= EDGES and NODES < NPAD and PADS <= CH

K_IOTA, K_H29, K_H32, K_H16, K_END = 0, LO4, LO4 + M1, LO4 + M1 + P, LO4 + M1 + 2 * P
Q_ID, Q_CNT, Q_SUM, Q_SQ, Q_B0, Q_B1, Q_S16 = 0, P, P + M1, P + 2 * M1, P + 3 * M1, 2 * P + 3 * M1, 3 * P + 3 * M1
Q_PAD4 = 4 * P + 3 * M1
Q_ISS, Q_PAD8, Q_END = Q_PAD4 + 1, Q_PAD4 + 2, Q_PAD4 + 3


def gnn_kernel(nc, x, dst, src, typ, attr, vec, w1, fcb, w2a, w2b, bn0, bn1, rw1, rr1, rb1, rw2, rr2, rb2,
               cst16, cst32, out):
    f32, bf16, f16, i32 = mybir.dt.float32, mybir.dt.bfloat16, mybir.dt.float16, mybir.dt.int32
    ALU, ACT, AX = mybir.AluOpType, mybir.ActivationFunctionType, mybir.AxisListType.X
    ds = bass.ds

    hid_d = nc.dram_tensor("hid_d", (GROUPS, HROWS, GROUP), f32, kind="Internal").ap()
    row_d = nc.dram_tensor("row_d", (NPAD, FT), f32, kind="Internal").ap()
    cidx_d = nc.dram_tensor("cidx_d", (P, TILES), i32, kind="Internal").ap()
    y1_d = nc.dram_tensor("y1_d", (NPAD * NREL, HID), f32, kind="Internal").ap()
    y2_d = nc.dram_tensor("y2_d", (NPAD * NREL, NS), f32, kind="Internal").ap()

    ctx = ExitStack()
    with ctx:
        def sb(name, shape, dt=f32):
            return ctx.enter_context(nc.sbuf_tensor(name, shape, dt))

        def sem(name):
            return ctx.enter_context(nc.semaphore(name))

        def sems(name):
            return [sem(f"{name}{b}") for b in range(2)]

        k16, k32 = sb("k16", [P, K_END], f16), sb("k32", [P, Q_END])
        w1_s, fcb_s = sb("w1_s", [P, H1AT + HROWS]), sb("fcb_s", [H1AT + HROWS, 1])
        w2a_s, w2b_s = sb("w2a_s", [H1AT + HROWS, NW1]), sb("w2b_s", [H1AT + HROWS, NW1])
        bn0_s, bn1_s = sb("bn0_s", [M1, 2]), sb("bn1_s", [P, 2])
        rb1_s, rb2_s = sb("rb1_s", [P, 1]), sb("rb2_s", [P, 1])
        rw1_s = sb("rw1_s", [P, 8, NREL * HID])
        rr1_s = sb("rr1_s", [P, 2, 4, HID])
        rw2_s = sb("rw2_s", [P, 4, NREL * NS])
        rr2_s = sb("rr2_s", [P, 2, 8, NS])
        src_i, dst_i, typ_i = sb("src_i", [P, TILES], i32), sb("dst_i", [P, TILES], i32), sb("typ_i", [P, TILES], i32)
        cidx_i = sb("cidx_i", [P, TILES], i32)
        typ_f = sb("typ_f", [P, TILES])
        s_hi4, s_lo4, s_hi8, s_lo8 = (sb(n, [P, TILES]) for n in ("s_hi4", "s_lo4", "s_hi8", "s_lo8"))
        d_hi4, d_lo4, d_hi8, d_lo8 = (sb(n, [P, TILES]) for n in ("d_hi4", "d_lo4", "d_hi8", "d_lo8"))
        d_lo16, d_seg, bit = sb("d_lo16", [P, TILES]), sb("d_seg", [P, TILES]), sb("bit", [P, TILES])
        early = sb("early", [P, TILES * NREL // 2])
        vec_s = early[:, 0:3 * TILES].rearrange("p (t c) -> p t c", c=3)
        tsel = early[:, :].bitcast(bf16).rearrange("p (t r) -> p t r", r=NREL)
        sh = sb("sh", [P, TILES, 3])
        norm = sb("norm", [P, TILES])
        we = sb("we", [P, TILES])
        ix = [sb(f"ix{b}", [P, TILE_G], i32) for b in range(2)]
        attr_s = [sb(f"attr{b}", [P, GROUP]) for b in range(2)]
        hid = [sb(f"hid{b}", [H1AT + HROWS, GROUP]) for b in range(2)]
        rows = [sb(f"rows{b}", [P, TILE_G * 40]) for b in range(2)]
        low = [sb(f"low{b}", [P, TILE_G, LO4], bf16) for b in range(2)]
        high = [sb(f"high{b}", [P, TILE_G * P], bf16) for b in range(2)]
        dist = sb("dist", [P, TILE_G * P], bf16)
        ldist = sb("ldist", [P, LOW_ACT, LO8], bf16)
        ddist = sb("ddist", [P, TILE_G, LO16], bf16)
        dlow = [sb(f"dlow{b}", [P, TILE_G, LO16], bf16) for b in range(2)]
        dseg = [sb(f"dseg{b}", [P, TILE_G, P], bf16) for b in range(2)]
        stk = [sb(f"stk{b}", [P, 3, TILE_G * P], bf16) for b in range(2)]
        prod = sb("prod", [P, 2, 2 * NW1])
        z = [sb(f"z{b}", [P, TILE_G, NS + NV]) for b in range(2)]
        msg = [sb(f"msg{b}", [P, TILE_G * HID]) for b in range(2)]
        part = sb("part", [P, 3, TILE_G * HID], bf16)
        rest = sb("rest", [P, TILE_G * HID])
        tmp4 = sb("tmp4", [P, TILE_G, NV])
        uvec = sb("uvec", [P, TILE_G, NV, 3])
        tval = sb("tval", [P, TILE_G, NREL])
        acc = sb("acc", [P, LO4])
        rec = sb("rec", [P, LO4])
        sq = sb("sq", [P, LO4])
        zeros = sb("zeros", [P, LO8], bf16)
        cdt = sb("cdt", [P, LO16])
        st = sb("st", [P, 8])
        r2 = sb("r2", [CH, NQ, FT])
        xr = sb("xr", [CH, C8, 8 * NS])
        x1 = sb("x1", [CH, C8, 8 * NS])
        x2 = sb("x2", [CH, C8, 8 * NS])
        x1t = sb("x1t", [P, LO8])
        ht = sb("ht", [P, LO4])
        ysb = sb("ysb", [CH, C8 * 8 * NREL * HID])
        lnm, lnv, lnr = sb("lnm", [CH, NQ]), sb("lnv", [CH, NQ]), sb("lnr", [CH, NQ])
        lnd = sb("lnd", [CH, NQ, NS])

        PS = ctx.enter_context(nc.psum_tensor("PS", [P, 8, 512], f32))
        ACC, CNT, HP, WP = 0, 2, 3, 4

        s_small, s_edge, s_x = sem("small_loaded"), sem("edge_arrays_loaded"), sem("x_rows_loaded")
        s_blk, s_zero = sem("block_weights_loaded"), sem("cleared")
        s_ix = [sems(f"index_loaded{n}_") for n in range(4)]
        s_gat = [sems(f"rows_gathered{n}_") for n in range(4)]
        s_in = [sems(f"net_input_loaded{n}_") for n in range(2)]
        s_hid, s_relu, s_hst = sem("hidden_made"), sem("hidden_rectified"), sems("hidden_stored")
        s_w = [sem(f"weights_made{n}") for n in range(2)]
        s_prod = [sem(f"products_made{n}") for n in range(2)]
        s_red = [sem(f"messages_made{n}") for n in range(4)]
        s_cast0 = [sem(f"first_part_cut{n}") for n in range(4)]
        s_cast1 = [sem(f"second_part_cut{n}") for n in range(4)]
        s_sub = [sem(f"rest_left{n}") for n in range(4)]
        s_mask = [sem(f"hi_onehot{n}") for n in range(4)]
        s_stk = [sem(f"stack_ready{n}") for n in range(4)]
        s_scat = [sem(f"group_summed{n}") for n in range(4)]
        s_z, s_u, s_t = sem("z_ready"), sem("u_ready"), sem("relation_weight")
        s_pre, s_sqrt, s_rt = sem("edge_arrays_made"), sem("norm_squared"), sem("norm_rooted")
        s_edge_made, s_cidx, s_node, s_pe, s_act = sem("per_edge_ready"), sem("cidx_stored"), sem("node_step"), sem("node_product"), sem("node_root")
        s_tab, s_ysb, s_out = sem("table_stored"), sem("table_rows_made"), sem("out_stored")
        s_go = sem("gather_may_start")
        s_late, s_yact, s_rest = sem("late_loaded"), sem("odd_table_rows_made"), sem("second_pass_arrays")
        s_clear, s_dif, s_hold = sem("operands_cleared"), [sem(f"distances_made{n}") for n in range(4)], sem("scalar_may_go")

        def k(col, n, rows_=P):
            return k32[0:rows_, col:col + n]

        HIGH = [(M1, K_H29, s_hi4), (P, K_H16, s_hi8), (P, K_H32, d_hi4), (P, K_H16, d_hi8)]
        LOW = [(s_lo4, LO4), (s_lo8, LO8), (d_lo4, LO4), (d_lo8, LO8)]
        MESSAGE = [F1, NS, HID, NS]
        REDUCTIONS = [5, 1, 1, 1]

        def groups(eng, step):
            step(0, 0)
            step(1, 1)
            with eng.Fori(1, STEPS) as i:
                step(2 * i, 0)
                step(2 * i + 1, 1)

        def pipelined(eng, step):
            step(0, 0)
            step(1, 1)
            with eng.Fori(1, STEPS - 1) as i:
                step(2 * i, 0)
                step(2 * i + 1, 1)
            step(GROUPS - 2, 0)
            step(GROUPS - 1, 1)

        def first(g, n=2):
            return isinstance(g, int) and g < n

        def last_group(g):
            return isinstance(g, int) and g == GROUPS - 1

        def turn(g, b):
            return g // 2 + 1 if isinstance(g, int) else (g - b) // 2 + 1

        block = ctx.enter_context(nc.Block())

        @block.sync
        def _(eng):
            eng.dma_start(vec_s, vec).then_inc(s_edge, 16)
            for t, s in ((typ_i, typ), (src_i, src), (dst_i, dst)):
                eng.dma_start(t[:, :], s).then_inc(s_edge, 16)
            eng.wait_ge(s_clear, 1)
            for t, s in ((k16, cst16), (w1_s[0:FD], w1), (fcb_s, fcb), (w2a_s[0:HROWS], w2a),
                         (w2b_s[H1AT:H1AT + HROWS], w2b)):
                eng.dma_start(t[:, :], s).then_inc(s_small, 16)

            def load_late():
                for t, s in ((k32, cst32), (bn0_s, bn0), (bn1_s, bn1), (rb1_s, rb1), (rb2_s, rb2)):
                    eng.dma_start(t[:, :], s).then_inc(s_late, 16)
                xv = x.rearrange("(h c p) f -> c p h f", c=C8, p=CH)
                for c in range(C8):
                    eng.dma_start(xr[:, c, :].rearrange("p (h f) -> p h f", h=8), xv[c]).then_inc(s_x, 16)
                eng.wait_ge(s_zero, 1)
                for h in range(8):
                    eng.dma_start(rw1_s[h * NS:(h + 1) * NS, h, :], rw1).then_inc(s_blk, 16)
                    eng.dma_start(rr1_s[h * NS:(h + 1) * NS, h % 2, h // 2, :], rr1).then_inc(s_blk, 16)
                    eng.dma_start(rr2_s[(h // 2) * HID:(h // 2 + 1) * HID, h % 2, h, :], rr2).then_inc(s_blk, 16)
                for h in range(4):
                    eng.dma_start(rw2_s[h * HID:(h + 1) * HID, h, :], rw2).then_inc(s_blk, 16)

            def load_ix(n, g, b, idx):
                if not first(g):
                    eng.wait_ge(s_gat[n][b], (turn(g, b) - 1) * (16 * TILE_G))
                at = ds(g * TILE_G, TILE_G) if not isinstance(g, int) else slice(g * TILE_G, (g + 1) * TILE_G)
                eng.dma_start(ix[b][:, :], idx[:, at]).then_inc(s_ix[n][b], 16)

            def pass1(g, b):
                load_ix(0, g, b, dst)
                if not first(g):
                    eng.wait_ge(s_hid, g - 1)
                at = ds(g * GROUP, GROUP) if not isinstance(g, int) else slice(g * GROUP, (g + 1) * GROUP)
                eng.dma_start(attr_s[b][0:FD, :], attr[:, at]).then_inc(s_in[0][b], 16)
            groups(eng, pass1)
            load_late()

            for b in range(2):
                eng.wait_ge(s_hst[b], 16 * STEPS)
                eng.wait_ge(s_gat[0][b], 16 * TILE_G * STEPS)

            def pass2(g, b):
                load_ix(1, g, b, dst)
                if not first(g):
                    eng.wait_ge(s_w[1], 2 * (g - 1))
                at = ds(g, 1) if not isinstance(g, int) else slice(g, g + 1)
                eng.dma_start(hid[b][H1AT:H1AT + HROWS, :], hid_d[at, :, :].rearrange("a k n -> k (a n)")).then_inc(s_in[1][b], 16)
            eng.wait_ge(s_w[0], 2 * GROUPS)
            groups(eng, pass2)

            eng.wait_ge(s_pre, 1)
            eng.dma_start(cidx_d, cidx_i[:, :]).then_inc(s_cidx, 16)
            eng.wait_ge(s_cidx, 16)
            for b in range(2):
                eng.wait_ge(s_gat[1][b], 16 * TILE_G * STEPS)
            yd = y1_d.rearrange("(h c p r) f -> c p h (r f)", h=8, c=C8, p=CH)
            for c in range(C8):
                eng.wait_ge(s_ysb, 2 * (c + 1))
                eng.wait_ge(s_yact, 2 * (c + 1))
                eng.dma_start(yd[c], ysb[:, c * 8 * NREL * HID:(c + 1) * 8 * NREL * HID]
                              .rearrange("p (h r) -> p h r", h=8)).then_inc(s_tab, 16)
            groups(eng, lambda g, b: load_ix(2, g, b, cidx_d))
            for b in range(2):
                eng.wait_ge(s_gat[2][b], 16 * TILE_G * STEPS)
            yd = y2_d.rearrange("(h c p r) f -> c p h (r f)", h=4, c=C4, p=CH)
            for c in range(C4):
                even, odd = Y1_EACH + c // 2 + 1, Y1_EACH + (c + 1) // 2
                eng.wait_ge(s_ysb, even)
                eng.wait_ge(s_yact, odd)
                eng.dma_start(yd[c], ysb[:, c * 512:(c + 1) * 512].rearrange("p (h r) -> p h r", h=4))\
                   .then_inc(s_tab, 16)
            groups(eng, lambda g, b: load_ix(3, g, b, cidx_d))

            eng.wait_ge(s_node, NODE_OUT)
            ov = out.rearrange("(h c p) f -> c p h f", c=C8, p=CH)
            for c in range(C8):
                eng.dma_start(ov[c], x2[:, c, :].rearrange("p (h f) -> p h f", h=8)).then_inc(s_out, 16)
            eng.wait_ge(s_out, 16 * C8)

        @block.gpsimd
        def _(eng):
            for t in (w1_s, w2a_s, w2b_s, attr_s[0], attr_s[1]):
                last = eng.memset(t[:, :], 0.0)
            last.then_inc(s_clear, 1)
            for t in (rw1_s, rw2_s):
                eng.memset(t[:, :, :], 0.0)
            for t in (rr1_s, rr2_s):
                last = eng.memset(t[:, :, :, :], 0.0)
            last.then_inc(s_zero, 1)
            eng.wait_ge(s_zero, 1)

            def gather(n, g, b, table, width, used):
                eng.wait_ge(s_ix[n][b], 16 * turn(g, b))
                if not first(g):
                    used(g)
                eng.sem_inc(s_go, 1)
                for u in range(TILE_G):
                    eng.indirect_dma_start(rows[b][:, u * width:(u + 1) * width], None, table,
                                           bass.IndirectOffsetOnAxis(ix[b][:, u:u + 1], 0)).then_inc(s_gat[n][b], 16)

            groups(eng, lambda g, b: gather(0, g, b, x, NS, lambda g: eng.wait_ge(s_prod[0], 2 * (g - 1))))
            eng.wait_ge(s_prod[0], 2 * GROUPS)
            eng.wait_ge(s_tab, 16)

            def used2(g):
                eng.wait_ge(s_z, g - 1)
                eng.wait_ge(s_t, 2 * (g - 1))
                eng.wait_ge(s_u, 2 * (g - 1))
            groups(eng, lambda g, b: gather(1, g, b, row_d, FT, used2))
            used2(GROUPS + 1)
            eng.wait_ge(s_tab, 16 * (1 + C8))
            groups(eng, lambda g, b: gather(2, g, b, y1_d, HID, lambda g: eng.wait_ge(s_red[2], g - 1)))
            eng.wait_ge(s_red[2], GROUPS)
            eng.wait_ge(s_tab, 16 * (1 + C8 + C4))
            groups(eng, lambda g, b: gather(3, g, b, y2_d, NS, lambda g: eng.wait_ge(s_red[3], g - 1)))

        @block.tensor
        def _(eng):
            mm = nc.tensor.matmul
            eng.wait_ge(s_small, 80)

            def scatter(n, g, b, cols, lo, halves):
                eng.wait_ge(s_stk[n], g + 1)
                for u in range(TILE_G):
                    for part_ in range(3):
                        for half in range(halves):
                            last = mm(PS[0:cols, ACC + half, 0:LO8], stk[b][:, part_, u * cols:(u + 1) * cols],
                                      low[b][:, u, half * LO8:(half + 1) * LO8], start=False, stop=True,
                                      skip_group_check=True)
                    if n == 0:
                        last = mm(PS[:, CNT, 0:LO16], dseg[b][:, u, :], dlow[b][:, u, :], start=False, stop=True,
                                  skip_group_check=True)
                last.then_inc(s_scat[n], 1)

            def make_hidden(g, b):
                eng.wait_ge(s_in[0][b], 16 * turn(g, b))
                if not (isinstance(g, int) and g == 0):
                    eng.wait_ge(s_relu, g)
                mm(PS[0:H1AT + HROWS, HP, :], w1_s[:, :], attr_s[b][:, :], start=True, stop=True).then_inc(s_hid, 1)

            def make_weights(n, g, w2, ready):
                b_ready, b = ready
                b_ready()
                for h in range(2):
                    if not (isinstance(g, int) and g == 0):
                        eng.wait_ge(s_prod[n], 2 * g - 1 + h)
                    for u in range(2):
                        last = mm(PS[:, WP + 2 * h + u, 0:NW1], hid[b][:, (2 * h + u) * P:(2 * h + u + 1) * P],
                                  w2[:, :], start=True, stop=True)
                    last.then_inc(s_w[n], 1)

            def step1(g, b):
                make_weights(0, g, w2a_s, (lambda: eng.wait_ge(s_relu, g + 1), b))
                if not last_group(g):
                    make_hidden(g + 1, 1 - b)
                if not first(g):
                    scatter(0, g - 2, b, M1, LO4, 2)

            eng.wait_ge(s_node, 1)
            for half in range(2):
                mm(PS[:, ACC + half, 0:LO8], zeros[:, 0:P], zeros[:, 0:LO8], start=True, stop=True, skip_group_check=True)
            mm(PS[:, CNT, 0:LO16], zeros[:, 0:P], zeros[:, 0:LO16], start=True, stop=True, skip_group_check=True)\
                .then_inc(s_scat[0], 1)
            make_hidden(0, 0)
            pipelined(eng, step1)
            for g in (GROUPS - 2, GROUPS - 1):
                scatter(0, g, g % 2, M1, LO4, 2)

            pe = [0]

            def done(ins):
                pe[0] += 1
                ins.then_inc(s_pe, 1)

            eng.wait_ge(s_late, 80)
            eng.wait_ge(s_node, 3)
            for half in range(2):
                last = mm(PS[0:M1, HP + half, 0:LO8], k(Q_CNT, M1, M1), acc[0:M1, half * LO8:(half + 1) * LO8],
                          start=True, stop=True)
            done(last)
            eng.wait_ge(s_node, NODE_SUM1)
            done(mm(PS[0:M1, 5, 0:1], k(Q_SUM, M1, M1), st[0:M1, 0:1], start=True, stop=True))
            eng.wait_ge(s_node, NODE_SQ1)
            done(mm(PS[0:M1, 6, 0:1], k(Q_SQ, M1, M1), st[0:M1, 2:3], start=True, stop=True))
            for half in range(2):
                last = mm(PS[:, 7, 0:LO8], k(Q_B0 + half * P, P, M1), rec[0:M1, half * LO8:(half + 1) * LO8],
                          start=half == 0, stop=half == 1)
            done(last)
            eng.wait_ge(s_node, NODE_BN1)
            for c in range(C4):
                last = nc.tensor.transpose(PS[0:CH, c // 4, (c % 4) * M1:(c % 4 + 1) * M1],
                                           acc[0:M1, c * CH:(c + 1) * CH], k(Q_ID, M1, M1))
            for c in range(C16):
                last = nc.tensor.transpose(PS[0:CH, 2, c * P:(c + 1) * P], cdt[:, c * CH:(c + 1) * CH], k(Q_ID, P))
            done(last)

            eng.wait_ge(s_node, NODE_ROWS1)
            mm(PS[:, ACC, 0:LO8], zeros[:, 0:P], zeros[:, 0:LO8], start=True, stop=True, skip_group_check=True)\
                .then_inc(s_scat[1], 1)

            def step2(g, b):
                make_weights(1, g, w2b_s, (lambda: eng.wait_ge(s_in[1][b], 16 * turn(g, b)), b))
                if not first(g):
                    scatter(1, g - 2, b, P, LO8, 1)
            groups(eng, step2)
            for g in (GROUPS - 2, GROUPS - 1):
                scatter(1, g, g % 2, P, LO8, 1)

            eng.wait_ge(s_node, NODE_SUM2)
            done(mm(PS[:, 5, 0:1], k(Q_S16, P), st[:, 0:1], start=True, stop=True))
            eng.wait_ge(s_node, NODE_SQ2)
            done(mm(PS[:, 6, 0:1], k(Q_S16, P), st[:, 2:3], start=True, stop=True))
            eng.wait_ge(s_node, NODE_BN2)
            for c in range(C8):
                last = nc.tensor.transpose(PS[0:CH, 2, c * P:(c + 1) * P], acc[:, c * CH:(c + 1) * CH], k(Q_ID, P))
            done(last)
            eng.wait_ge(s_node, NODE_X1)
            for c in range(C8):
                last = nc.tensor.transpose(PS[:, 3, c * CH:(c + 1) * CH], x1[:, c, :], k(Q_ID, CH, CH))
            done(last)
            eng.wait_ge(s_node, NODE_X1T)
            eng.wait_ge(s_blk, 16 * 28)
            for half in range(2):
                last = mm(PS[:, ACC + half, 0:LO8], rr1_s[:, half, :, :].rearrange("p h f -> p (h f)"), x1t[:, :],
                          start=True, stop=True, skip_group_check=True)
            last.then_inc(s_scat[2], 1)
            for n in range(4 * C8):
                if n >= 4:
                    eng.wait_ge(s_yact if n % 2 else s_ysb, n // 2 - 1)
                done(mm(PS[0:CH, 4 + n % 4, :], x1t[:, (n // 4) * CH:(n // 4 + 1) * CH],
                        rw1_s[:, 2 * (n % 4):2 * (n % 4) + 2, :].rearrange("p h r -> p (h r)"), start=True, stop=True))
            groups(eng, lambda g, b: scatter(2, g, b, P, LO4, 2))

            eng.wait_ge(s_act, ACT_H)
            for half in range(2):
                last = mm(PS[:, 2, 0:LO8], rr2_s[:, half, :, :].rearrange("p h f -> p (h f)"),
                          ht[:, half * LO8:(half + 1) * LO8], start=half == 0, stop=half == 1, skip_group_check=True)
            last.then_inc(s_scat[3], 1)
            for n in range(C4):
                eng.wait_ge(s_yact if n % 2 else s_ysb, Y1_EACH + n // 2 - 1)
                done(mm(PS[0:CH, 4 + n % 4, :], ht[:, n * CH:(n + 1) * CH], rw2_s[:, :, :].rearrange("p h r -> p (h r)"),
                        start=True, stop=True))

            def scatter4(g, b):
                eng.wait_ge(s_stk[3], g + 1)
                for u in range(TILE_G):
                    for part_ in range(3):
                        last = mm(PS[:, 2, 0:LO8], stk[b][:, part_, u * P:(u + 1) * P], low[b][:, u, 0:LO8],
                                  start=False, stop=True, skip_group_check=True)
                last.then_inc(s_scat[3], 1)
            groups(eng, scatter4)
            eng.wait_ge(s_node, NODE_B2)
            for c in range(C8):
                last = nc.tensor.transpose(PS[0:CH, 3, c * P:(c + 1) * P], acc[:, c * CH:(c + 1) * CH], k(Q_ID, P))
            done(last)
            assert pe[0] == PE_OUT

        @block.scalar
        def _(eng):
            act = nc.scalar.activation
            shf = sh[:, :, :].rearrange("p t c -> p (t c)")
            eng.wait_ge(s_edge, 64)
            act(shf, early[:, 0:3 * TILES], ACT.Square).then_inc(s_rt, 1)
            eng.wait_ge(s_sqrt, 2)
            act(norm[:, :], norm[:, :], ACT.Sqrt).then_inc(s_rt, 1)
            eng.wait_ge(s_small, 80)

            def tile(g, u):
                return ds(g * TILE_G + u, 1) if not isinstance(g, int) else slice(g * TILE_G + u, g * TILE_G + u + 1)

            def distances(n, g):
                cols, kcol, hi = HIGH[n]
                if not first(g, 1):
                    eng.wait_ge(s_mask[n], g)
                eng.sem_inc(s_hold, 1)
                for u in range(TILE_G):
                    last = act(dist[:, u * cols:(u + 1) * cols], k16[:, kcol:kcol + cols], ACT.Abs,
                               bias=hi[:, tile(g, u)], scale=-1.0)
                    if n == 0:
                        last = act(ddist[:, u, :], k16[:, K_IOTA:K_IOTA + LO16], ACT.Abs,
                                   bias=d_lo16[:, tile(g, u)], scale=-1.0)
                    if n == 1 and u < LOW_ACT:
                        last = act(ldist[:, u, :], k16[:, K_IOTA:K_IOTA + LO8], ACT.Abs,
                                   bias=s_lo8[:, tile(g, u)], scale=-1.0)
                last.then_inc(s_dif[n], 1)

            def masks(n, g, b):
                cols = HIGH[n][0]
                if not first(g):
                    eng.wait_ge(s_scat[n], g)
                eng.wait_ge(s_dif[n], g + 1)
                if n == 0:
                    act(dlow[b][:, :, :], ddist[:, :, :], ACT.Relu, bias=1.0, scale=-1.0)
                if n == 1:
                    act(low[b][:, 0:LOW_ACT, 0:LO8], ldist[:, :, :], ACT.Relu, bias=1.0, scale=-1.0)
                act(high[b][:, 0:TILE_G * cols], dist[:, 0:TILE_G * cols], ACT.Relu, bias=1.0, scale=-1.0)\
                    .then_inc(s_mask[n], 1)

            def casts(n, g, b):
                w = TILE_G * MESSAGE[n]
                eng.wait_ge(s_red[n], (g + 1) * REDUCTIONS[n])
                if not first(g, 1):
                    eng.wait_ge(s_stk[n], g)
                act(part[:, 0, 0:w], msg[b][:, 0:w], ACT.Copy).then_inc(s_cast0[n], 1)
                eng.wait_ge(s_sub[n], 2 * g + 1)
                act(part[:, 1, 0:w], rest[:, 0:w], ACT.Copy).then_inc(s_cast1[n], 1)

            def behind(n, g, b):
                if not first(g, 1):
                    casts(n, g - 1, 1 - b)
                    masks(n, g - 1, 1 - b)

            def finish(n):
                casts(n, GROUPS - 1, 1)
                masks(n, GROUPS - 1, 1)

            eng.wait_ge(s_edge_made, 1)
            act(shf, shf, ACT.Copy, scale=3.0 ** 0.5).then_inc(s_rt, 1)

            def rectify(g, b):
                eng.wait_ge(s_hid, g + 1)
                if not first(g):
                    eng.wait_ge(s_w[0], 2 * (g - 1))
                    eng.wait_ge(s_hst[b], 16 * (turn(g, b) - 1))
                act(hid[b][:, :], PS[0:H1AT + HROWS, HP, :], ACT.Relu, bias=fcb_s[:, 0:1]).then_inc(s_relu, 1)

            def store_hidden(g, b):
                eng.wait_ge(s_relu, g + 1)
                at = ds(g, 1) if not isinstance(g, int) else slice(g, g + 1)
                eng.dma_start(hid_d[at, :, :].rearrange("a k n -> k (a n)"), hid[b][H1AT:H1AT + HROWS, :])\
                   .then_inc(s_hst[b], 16)

            def pass1(g, b):
                behind(0, g, b)
                if not last_group(g):
                    rectify(g + 1, 1 - b)
                distances(0, g)
                if not last_group(g):
                    store_hidden(g + 1, 1 - b)
            rectify(0, 0)
            store_hidden(0, 0)
            pipelined(eng, pass1)
            finish(0)

            def root(n, value):
                eng.wait_ge(s_node, value)
                act(st[0:n, 3:4], st[0:n, 3:4], ACT.Sqrt).then_inc(s_act, 1)
            root(M1, NODE_VAR1)
            act(shf, shf, ACT.Copy, scale=3.0 ** -0.5).then_inc(s_rt, 1)
            eng.wait_ge(s_node, NODE_ROWS1)
            eng.dma_start(row_d.rearrange("(q p) f -> p q f", p=CH), r2[:, :, :]).then_inc(s_tab, 16)

            def scalars_in(g, b):
                eng.wait_ge(s_gat[1][b], 16 * TILE_G * turn(g, b))
                if not first(g):
                    eng.wait_ge(s_prod[1], 2 * (g - 1))
                rv = rows[b][:, 0:TILE_G * FT].rearrange("p (t f) -> p t f", f=FT)
                act(z[b][:, :, 0:NS], rv[:, :, 0:NS], ACT.Copy).then_inc(s_z, 1)

            def pass2(g, b):
                behind(1, g, b)
                if not last_group(g):
                    scalars_in(g + 1, 1 - b)
                distances(1, g)
            scalars_in(0, 0)
            eng.wait_ge(s_rest, 1)
            pipelined(eng, pass2)
            finish(1)
            root(P, NODE_VAR2)
            eng.wait_ge(s_node, NODE_LN1)
            act(lnr[:, :], lnv[:, :], ACT.Sqrt).then_inc(s_act, 1)
            y1v = ysb[:, :].rearrange("p (n m) -> p n m", m=512)

            def odd_rows(count, before):
                for n in range(1, count, 2):
                    eng.wait_ge(s_pe, before + n + 1)
                    act(y1v[:, n, :], PS[0:CH, 4 + n % 4, :], ACT.Copy).then_inc(s_yact, 1)
            odd_rows(4 * C8, 9)

            def relational(n):
                def step(g, b):
                    behind(n, g, b)
                    distances(n, g)
                pipelined(eng, step)
                finish(n)
            relational(2)
            eng.wait_ge(s_scat[2], 1 + GROUPS)
            for half in range(2):
                last = act(ht[:, half * LO8:(half + 1) * LO8], PS[:, ACC + half, 0:LO8], ACT.Relu, bias=rb1_s[:, 0:1])
            last.then_inc(s_act, 1)
            eng.wait_ge(s_tab, 16 * (1 + C8))
            odd_rows(C4, 9 + 4 * C8)
            relational(3)
            eng.wait_ge(s_node, NODE_LN2)
            act(lnr[:, :], lnv[:, :], ACT.Sqrt).then_inc(s_act, 1)
            eng.wait_ge(s_tab, 16 * (1 + C8 + C4))

        @block.vector
        def _(eng):
            v = nc.vector
            node = [0]

            def link(ins):
                node[0] += 1
                ins.then_inc(s_node, 1)
                eng.wait_ge(s_node, node[0])

            def at(name, value):
                assert node[0] == value, (name, node[0])

            link(v.memset(zeros[:, :], 0.0))
            for b in range(2):
                last = v.memset(msg[b][:, :], 1.0)
            link(last)
            eng.wait_ge(s_edge, 64)
            chain = [0]

            def step(ins):
                chain[0] += 1
                ins.then_inc(s_sqrt, 1)
                eng.wait_ge(s_sqrt, chain[0])

            step(v.tensor_copy(typ_f[:, :], typ_i[:, :]))
            eng.wait_ge(s_rt, 1)
            step(v.tensor_reduce(norm[:, :], sh[:, :, :], AX, ALU.add))
            def split4(i, hi4, lo4):
                step(v.tensor_copy(lo4[:, :], i[:, :]))
                step(v.tensor_scalar(hi4[:, :], lo4[:, :], float(LO4), None, ALU.is_ge))
                for m in (2, 3):
                    step(v.scalar_tensor_tensor(hi4[:, :], lo4[:, :], float(m * LO4), hi4[:, :], ALU.is_ge, ALU.add))
                step(v.scalar_tensor_tensor(lo4[:, :], hi4[:, :], -float(LO4), lo4[:, :], ALU.mult, ALU.add))

            def split8(hi4, lo4, hi8, lo8):
                step(v.tensor_scalar(bit[:, :], lo4[:, :], float(LO8), None, ALU.is_ge))
                step(v.scalar_tensor_tensor(hi8[:, :], hi4[:, :], 2.0, bit[:, :], ALU.mult, ALU.add))
                step(v.scalar_tensor_tensor(lo8[:, :], bit[:, :], -float(LO8), lo4[:, :], ALU.mult, ALU.add))
            split4(src_i, s_hi4, s_lo4)
            eng.wait_ge(s_rt, 2)
            step(v.tensor_scalar(norm[:, :], norm[:, :], 1e-12, None, ALU.add))
            step(v.reciprocal(norm[:, :], norm[:, :]))
            step(v.tensor_tensor(sh[:, :, :], vec_s, norm[:, :].unsqueeze(2).broadcast_to([P, TILES, 3]), ALU.mult))
            split4(dst_i, d_hi4, d_lo4)
            split8(d_hi4, d_lo4, d_hi8, d_lo8)
            step(v.tensor_scalar(bit[:, :], d_lo8[:, :], float(LO16), None, ALU.is_ge))
            step(v.scalar_tensor_tensor(d_lo16[:, :], bit[:, :], -float(LO16), d_lo8[:, :], ALU.mult, ALU.add))
            step(v.scalar_tensor_tensor(d_seg[:, :], d_hi8[:, :], 2.0, bit[:, :], ALU.mult, ALU.add))
            v.scalar_tensor_tensor(d_seg[:, :], d_seg[:, :], float(NREL), typ_f[:, :], ALU.mult, ALU.add)\
             .then_inc(s_edge_made, 1)
            eng.wait_ge(s_edge_made, 1)

            def later_arrays():
                split8(s_hi4, s_lo4, s_hi8, s_lo8)
                v.tensor_tensor(tsel, k16[:, K_IOTA:K_IOTA + NREL].unsqueeze(1).broadcast_to([P, TILES, NREL]),
                                typ_f[:, :].unsqueeze(2).broadcast_to([P, TILES, NREL]), ALU.is_equal)\
                 .then_inc(s_rest, 1)
                step(v.tensor_copy(bit[:, :], src_i[:, :]))
                step(v.scalar_tensor_tensor(bit[:, :], bit[:, :], float(NREL), typ_f[:, :], ALU.mult, ALU.add))
                v.tensor_copy(cidx_i[:, :], bit[:, :]).then_inc(s_pre, 1)
                eng.wait_ge(s_rest, 1)

            eng.wait_ge(s_small, 80)
            eng.wait_ge(s_rt, 3)

            def tile(g, u):
                return ds(g * TILE_G + u, 1) if not isinstance(g, int) else slice(g * TILE_G + u, g * TILE_G + u + 1)

            def tiles(g):
                return ds(g * TILE_G, TILE_G) if not isinstance(g, int) else slice(g * TILE_G, (g + 1) * TILE_G)

            def first_rest(n, g, b):
                w = TILE_G * MESSAGE[n]
                eng.wait_ge(s_cast0[n], g + 1)
                v.tensor_tensor(rest[:, 0:w], msg[b][:, 0:w], part[:, 0, 0:w], ALU.subtract).then_inc(s_sub[n], 1)

            def second_rest(n, g, b):
                w = TILE_G * MESSAGE[n]
                eng.wait_ge(s_cast1[n], g + 1)
                v.tensor_tensor(part[:, 2, 0:w], rest[:, 0:w], part[:, 1, 0:w], ALU.subtract).then_inc(s_sub[n], 1)
                if not first(g):
                    eng.wait_ge(s_scat[n], g)
                lo, width = LOW[n]
                for u in range(TILE_G):
                    if n == 0:
                        v.tensor_scalar(dseg[b][:, u, :], k16[:, K_IOTA:K_IOTA + P], d_seg[:, tile(g, u)], None,
                                        ALU.is_equal)
                    if n != 1 or u >= LOW_ACT:
                        v.tensor_scalar(low[b][:, u, 0:width], k16[:, K_IOTA:K_IOTA + width], lo[:, tile(g, u)], None,
                                        ALU.is_equal)

            def stack(n, g, b):
                f, w = MESSAGE[n], TILE_G * MESSAGE[n]
                a = HIGH[n][0] // f
                eng.wait_ge(s_mask[n], g + 1)
                eng.wait_ge(s_sub[n], 2 * g + 2)
                for m in range(3):
                    last = v.tensor_tensor(
                        stk[b][:, m, 0:w * a].rearrange("p (t h f) -> p t h f", h=a, f=f),
                        high[b][:, 0:w * a].rearrange("p (t h f) -> p t h f", h=a, f=f),
                        part[:, m, 0:w].rearrange("p (t f) -> p t f", f=f).unsqueeze(2).broadcast_to([P, TILE_G, a, f]),
                        ALU.mult)
                last.then_inc(s_stk[n], 1)

            def finish(n):
                first_rest(n, GROUPS - 1, 1)
                second_rest(n, GROUPS - 1, 1)
                stack(n, GROUPS - 1, 1)

            def products(n, g, h, x_in, nj, ni):
                eng.wait_ge(s_w[n], 2 * g + 1 + h)
                v.tensor_tensor(prod[:, h, :].rearrange("p (t j i) -> p t j i", t=2, j=nj),
                                PS[:, WP + 2 * h:WP + 2 * h + 2, 0:NW1].rearrange("p t (j i) -> p t j i", j=nj),
                                x_in[:, 2 * h:2 * h + 2, :].unsqueeze(2).broadcast_to([P, 2, nj, ni]),
                                ALU.mult).then_inc(s_prod[n], 1)

            def pass1(g, b):
                if not first(g, 1):
                    first_rest(0, g - 1, 1 - b)
                eng.wait_ge(s_gat[0][b], 16 * TILE_G * turn(g, b))
                xg = rows[b][:, 0:TILE_G * NS].rearrange("p (t f) -> p t f", f=NS)
                mv = msg[b][:, 0:TILE_G * F1].rearrange("p (t f) -> p t f", f=F1)
                for h in range(2):
                    products(0, g, h, xg, NS + NV, NS)
                if not first(g, 1):
                    second_rest(0, g - 1, 1 - b)
                for h in range(2):
                    eng.wait_ge(s_prod[0], 2 * g + 1 + h)
                    pv = prod[:, h, :].rearrange("p (t j i) -> p t j i", t=2, j=NS + NV)
                    v.tensor_reduce(tmp4[:, 2 * h:2 * h + 2, :], pv[:, :, NS:NS + NV, :], AX, ALU.add).then_inc(s_red[0], 1)
                    v.tensor_reduce(mv[:, 2 * h:2 * h + 2, 0:NS], pv[:, :, 0:NS, :], AX, ALU.add).then_inc(s_red[0], 1)
                if not first(g, 1):
                    stack(0, g - 1, 1 - b)
                eng.wait_ge(s_red[0], 5 * g + 4)
                v.tensor_tensor(mv[:, :, NS:NS + 3 * NV].rearrange("p t (j c) -> p t j c", c=3),
                                tmp4[:, :, :].unsqueeze(3).broadcast_to([P, TILE_G, NV, 3]),
                                sh[:, tiles(g), :].unsqueeze(2).broadcast_to([P, TILE_G, NV, 3]),
                                ALU.mult).then_inc(s_red[0], 1)
            groups(eng, pass1)
            finish(0)

            at("start", 2)
            eng.wait_ge(s_scat[0], 1 + GROUPS)
            link(v.tensor_copy(acc[0:M1, :].rearrange("p (a n) -> p a n", a=2), PS[0:M1, ACC:ACC + 2, 0:LO8]))
            link(v.tensor_scalar(cdt[:, :], PS[:, CNT, 0:LO16], 1.0, None, ALU.max))
            link(v.reciprocal(cdt[:, :], cdt[:, :]))
            eng.wait_ge(s_pe, 1)
            link(v.tensor_scalar(rec[0:M1, :].rearrange("p (a n) -> p a n", a=2), PS[0:M1, HP:HP + 2, 0:LO8], 1.0, None,
                                 ALU.max))
            link(v.reciprocal(rec[0:M1, :], rec[0:M1, :]))
            link(v.scalar_tensor_tensor(acc[0:M1, :], acc[0:M1, :], NS ** -0.5, rec[0:M1, :], ALU.mult, ALU.mult))

            def batch_norm(n, width, bank_sum, pe_sum, pad_col, only, bn, n_act):
                def clear_pads():
                    link(v.tensor_scalar(acc[0:n, width - PADS:width], acc[0:n, width - PADS:width],
                                         k(pad_col, 1, n), None, ALU.mult))
                clear_pads()
                link(v.tensor_reduce(st[0:n, 0:1], acc[0:n, 0:width], AX, ALU.add))
                yield
                eng.wait_ge(s_pe, pe_sum)
                if only is None:
                    link(v.tensor_scalar(st[0:n, 1:2], PS[0:n, 5, 0:1], 1.0 / NODES, None, ALU.mult))
                else:
                    link(v.tensor_scalar(st[0:n, 1:2], PS[0:n, 5, 0:1], k(only, 1, n), 1.0 / NODES, ALU.mult, ALU.mult))
                link(v.tensor_scalar(acc[0:n, 0:width], acc[0:n, 0:width], st[0:n, 1:2], None, ALU.subtract))
                clear_pads()
                link(v.tensor_tensor(sq[0:n, 0:width], acc[0:n, 0:width], acc[0:n, 0:width], ALU.mult))
                link(v.tensor_reduce(st[0:n, 2:3], sq[0:n, 0:width], AX, ALU.add))
                yield
                eng.wait_ge(s_pe, pe_sum + 1)
                link(v.tensor_scalar(st[0:n, 3:4], PS[0:n, 6, 0:1], 1.0 / NODES, EPS, ALU.mult, ALU.add))
                yield
                eng.wait_ge(s_act, n_act)
                link(v.reciprocal(st[0:n, 4:5], st[0:n, 3:4]))
                link(v.tensor_tensor(st[0:n, 4:5], st[0:n, 4:5], bn[0:n, 0:1], ALU.mult))
                link(v.tensor_scalar(acc[0:n, 0:width], acc[0:n, 0:width], st[0:n, 4:5], bn[0:n, 1:2], ALU.mult, ALU.add))
                yield
            stage = batch_norm(M1, LO4, 5, 2, Q_PAD4, Q_ISS, bn0_s, 1)
            for name, value in (("sum", NODE_SUM1), ("sq", NODE_SQ1), ("var", NODE_VAR1), ("bn", NODE_BN1)):
                next(stage)
                at(name, value)
            eng.wait_ge(s_pe, 5)
            r2v = r2[:, :, 0:FT - NREL].rearrange("p (h c) f -> p c h f", h=4)
            for c in range(C4):
                link(v.tensor_copy(r2v[:, c], PS[0:CH, c // 4, (c % 4) * M1:(c % 4 + 1) * M1]
                                   .rearrange("p (h f) -> p h f", h=4)[:, :, 0:F1 - 1]))
            r2c = r2[:, :, FT - NREL:FT].rearrange("p (h c) f -> p c h f", h=16)
            for c in range(C16):
                link(v.tensor_copy(r2c[:, c], PS[0:CH, 2, c * P:(c + 1) * P].rearrange("p (h f) -> p h f", h=16)))
            link(v.tensor_copy(rec[:, 0:LO8], PS[:, 7, 0:LO8]))
            at("rows1", NODE_ROWS1)
            later_arrays()
            eng.wait_ge(s_rt, 4)

            def gathered2(g, b):
                eng.wait_ge(s_gat[1][b], 16 * TILE_G * turn(g, b))
                rv = rows[b][:, 0:TILE_G * FT].rearrange("p (t f) -> p t f", f=FT)
                v.tensor_tensor(uvec[:, :, :, :], rv[:, :, NS:NS + 3 * NV].rearrange("p t (j c) -> p t j c", c=3),
                                sh[:, tiles(g), :].unsqueeze(2).broadcast_to([P, TILE_G, NV, 3]), ALU.mult).then_inc(s_u, 1)
                v.tensor_tensor(tval[:, :, :], tsel[:, tiles(g), :], rv[:, :, FT - NREL:FT], ALU.mult).then_inc(s_t, 1)
                eng.wait_ge(s_u, 2 * g + 1)
                v.tensor_reduce(z[b][:, :, NS:NS + NV], uvec[:, :, :, :], AX, ALU.add).then_inc(s_u, 1)
                eng.wait_ge(s_t, 2 * g + 1)
                v.tensor_reduce(we[:, tiles(g)], tval[:, :, :], AX, ALU.add).then_inc(s_t, 1)

            def pass2(g, b):
                if not first(g, 1):
                    first_rest(1, g - 1, 1 - b)
                eng.wait_ge(s_u, 2 * g + 2)
                eng.wait_ge(s_z, g + 1)
                mv = msg[b][:, 0:TILE_G * NS].rearrange("p (t f) -> p t f", f=NS)
                for h in range(2):
                    products(1, g, h, z[b], NS, NS + NV)
                if not first(g, 1):
                    second_rest(1, g - 1, 1 - b)
                for h in range(2):
                    eng.wait_ge(s_prod[1], 2 * g + 1 + h)
                    pv = prod[:, h, :].rearrange("p (t j i) -> p t j i", t=2, j=NS)
                    last = v.tensor_reduce(mv[:, 2 * h:2 * h + 2, :], pv, AX, ALU.add)
                last.then_inc(s_red[1], 1)
                if not first(g, 1):
                    stack(1, g - 1, 1 - b)
                if not last_group(g):
                    gathered2(g + 1, 1 - b)
            gathered2(0, 0)
            pipelined(eng, pass2)
            finish(1)

            eng.wait_ge(s_scat[1], 1 + GROUPS)
            link(v.scalar_tensor_tensor(acc[:, 0:LO8], PS[:, ACC, 0:LO8], (NS + NV) ** -0.5, rec[:, 0:LO8],
                                        ALU.mult, ALU.mult))
            stage = batch_norm(P, LO8, 5, 6, Q_PAD8, None, bn1_s, 2)
            for name, value in (("sum", NODE_SUM2), ("sq", NODE_SQ2), ("var", NODE_VAR2), ("bn", NODE_BN2)):
                next(stage)
                at(name, value)

            def layer_norm(bank, plus, to, n_act):
                d = lnd[:, :, :].rearrange("p q f -> p (q f)")
                link(v.tensor_tensor(to[:, :, :].rearrange("p c n -> p (c n)"), PS[0:CH, bank, :],
                                     plus[:, :, :].rearrange("p c n -> p (c n)"), ALU.add))
                tv = to[:, :, :].rearrange("p c (h f) -> p (c h) f", f=NS)
                wide = [CH, NQ, NS]
                link(v.tensor_reduce(lnm[:, :], tv, AX, ALU.add))
                link(v.tensor_scalar(lnm[:, :], lnm[:, :], 1.0 / NS, None, ALU.mult))
                link(v.tensor_tensor(tv, tv, lnm[:, :].unsqueeze(2).broadcast_to(wide), ALU.subtract))
                link(v.tensor_tensor(lnd[:, :, :], tv, tv, ALU.mult))
                link(v.tensor_reduce(lnv[:, :], lnd[:, :, :], AX, ALU.add))
                link(v.tensor_scalar(lnv[:, :], lnv[:, :], 1.0 / NS, EPS, ALU.mult, ALU.add))
                yield
                eng.wait_ge(s_act, n_act)
                link(v.reciprocal(lnr[:, :], lnr[:, :]))
                link(v.tensor_tensor(tv, tv, lnr[:, :].unsqueeze(2).broadcast_to(wide), ALU.mult))
                yield
            eng.wait_ge(s_pe, 8)
            eng.wait_ge(s_x, 16 * C8)
            stage = layer_norm(2, xr, x1, 3)
            next(stage)
            at("ln1", NODE_LN1)
            next(stage)
            at("x1", NODE_X1)
            eng.wait_ge(s_pe, 9)
            link(v.tensor_copy(x1t[:, :], PS[:, 3, 0:LO8]))
            at("x1t", NODE_X1T)
            y1v = ysb[:, :].rearrange("p (n m) -> p n m", m=512)
            for n in range(0, 4 * C8, 2):
                eng.wait_ge(s_pe, 10 + n)
                v.tensor_copy(y1v[:, n, :], PS[0:CH, 4 + n % 4, :]).then_inc(s_ysb, 1)

            def relational(n):
                f = MESSAGE[n]

                def step(g, b):
                    eng.wait_ge(s_gat[n][b], 16 * TILE_G * turn(g, b))
                    v.tensor_tensor(msg[b][:, 0:TILE_G * f].rearrange("p (t f) -> p t f", f=f),
                                    rows[b][:, 0:TILE_G * f].rearrange("p (t f) -> p t f", f=f),
                                    we[:, tiles(g)].unsqueeze(2).broadcast_to([P, TILE_G, f]), ALU.mult).then_inc(s_red[n], 1)
                    if not first(g, 1):
                        first_rest(n, g - 1, 1 - b)
                        second_rest(n, g - 1, 1 - b)
                        stack(n, g - 1, 1 - b)
                groups(eng, step)
                finish(n)
            relational(2)
            eng.wait_ge(s_tab, 16 * (1 + C8))
            for n in range(0, C4, 2):
                eng.wait_ge(s_pe, 10 + 4 * C8 + n)
                v.tensor_copy(y1v[:, n, :], PS[0:CH, 4 + n % 4, :]).then_inc(s_ysb, 1)
            relational(3)
            eng.wait_ge(s_scat[3], 1 + GROUPS)
            link(v.tensor_scalar(acc[:, 0:LO8], PS[:, 2, 0:LO8], rb2_s[:, 0:1], None, ALU.add))
            at("b2", NODE_B2)
            eng.wait_ge(s_pe, PE_OUT)
            stage = layer_norm(3, x1, x2, 5)
            next(stage)
            at("ln2", NODE_LN2)
            next(stage)
            at("out", NODE_OUT)


NODE_SUM1 = 10
NODE_SQ1 = NODE_SUM1 + 5
NODE_VAR1 = NODE_SQ1 + 1
NODE_BN1 = NODE_VAR1 + 3
NODE_ROWS1 = NODE_BN1 + C4 + C16 + 1
NODE_SUM2 = NODE_ROWS1 + 3
NODE_SQ2 = NODE_SUM2 + 5
NODE_VAR2 = NODE_SQ2 + 1
NODE_BN2 = NODE_VAR2 + 3
NODE_LN1 = NODE_BN2 + 7
NODE_X1 = NODE_LN1 + 2
NODE_X1T = NODE_X1 + 1
NODE_B2 = NODE_X1T + 1
NODE_LN2 = NODE_B2 + 7
NODE_OUT = NODE_LN2 + 2
ACT_H = 4
PE_OUT = 9 + 4 * C8 + C4 + 1


def _constants(np):
    row = np.concatenate([np.arange(LO4), np.repeat(np.arange(4), F1), np.repeat(np.arange(4), HID),
                          np.repeat(np.arange(8), NS)])
    c16 = np.ascontiguousarray(np.broadcast_to(row.astype(np.float16), (P, K_END)))
    c32 = np.zeros((P, Q_END), np.float32)
    q, m = np.arange(M1)[:, None], np.arange(M1)[None, :]
    qf, mf = q % F1, m % F1
    c32[:, Q_ID:Q_ID + P] = np.eye(P)
    c32[:M1, Q_CNT:Q_CNT + M1] = (qf == F1 - 1) & (q // F1 == m // F1)
    c32[:M1, Q_SUM:Q_SUM + M1] = qf == mf
    both = (qf >= NS) & (mf >= NS) & (qf < F1 - 1) & (mf < F1 - 1) & ((qf - NS) // 3 == (mf - NS) // 3)
    c32[:M1, Q_SQ:Q_SQ + M1] = np.where(qf < NS, qf == mf, both / 3)
    wide = np.arange(P)[None, :]
    for b in range(2):
        c32[:M1, Q_B0 + b * P:Q_B0 + (b + 1) * P] = (qf == F1 - 1) & (wide // NS == 2 * (q // F1) + b)
    c32[:, Q_S16:Q_S16 + P] = np.arange(P)[:, None] % NS == wide % NS
    c32[:M1, Q_PAD4] = np.arange(M1) // F1 < 3
    c32[:M1, Q_ISS] = np.arange(M1) % F1 < NS
    c32[:, Q_PAD8] = np.arange(P) // NS < 7
    return c16, c32


def kernel(**inputs):
    import numpy as np
    import concourse.bacc as bacc
    from concourse.bass_utils import run_bass_kernel_spmd

    a = {n: np.asarray(v) for n, v in inputs.items()}
    slots = TILES * P

    def edges(v, fill):
        full = np.full((slots,) + v.shape[1:], fill, v.dtype)
        full[:EDGES] = v
        return np.ascontiguousarray(full.reshape((TILES, P) + v.shape[1:]).swapaxes(0, 1))

    x = np.zeros((NPAD, NS), np.float32)
    x[:NODES] = a["x"]
    attr = np.zeros((FD, slots), np.float32)
    attr[:, :EDGES] = a["edge_attr_48"].T
    w1 = np.zeros((FD, H1AT + HROWS), np.float32)
    fcb = np.zeros((H1AT + HROWS, 1), np.float32)
    for n, at in ((0, 0), (1, H1AT)):
        w1[:, at:at + FD] = a[f"L0_gnn_fc{n}_w1"]
        fcb[at:at + FD, 0] = a[f"L0_gnn_fc{n}_b1"]
        fcb[at + FD, 0] = 1

    def weights(n):
        w = np.concatenate([a[f"L0_gnn_fc{n}_w2"], a[f"L0_gnn_fc{n}_b2"][None]])
        s, v = w[:, :NS * NS].reshape(HROWS, NS, NS), w[:, NS * NS:]
        if n == 0:
            w = np.concatenate([s, v.reshape(HROWS, NS, NV)], 2)
        else:
            w = np.concatenate([s, v.reshape(HROWS, NV, NS)], 1)
        return np.ascontiguousarray(w.transpose(0, 2, 1).reshape(HROWS, NW1))

    bn0 = np.zeros((4, F1, 2), np.float32)
    bn0[:, :NS, 0], bn0[:, :NS, 1] = a["L0_gnn_bn0_gs"], a["L0_gnn_bn0_bs"]
    bn0[:, NS:F1 - 1, 0] = np.repeat(a["L0_gnn_bn0_gv"], 3)
    bn1 = np.tile(np.stack([a["L0_gnn_bn1_gs"], a["L0_gnn_bn1_bs"]], 1), (8, 1))
    c16, c32 = _constants(np)
    arrays = {
        "x": x, "dst": edges(a["dst"], NODES), "src": edges(a["src"], NODES), "typ": edges(a["edge_type_8"], 0),
        "attr": attr, "vec": edges(a["edge_attr_3"], 0), "w1": w1, "fcb": fcb, "w2a": weights(0), "w2b": weights(1),
        "bn0": bn0.reshape(M1, 2), "bn1": bn1,
        "rw1": np.ascontiguousarray(a["L1_gnn_W1"].transpose(1, 0, 2).reshape(NS, NREL * HID)),
        "rr1": a["L1_gnn_root1"], "rb1": np.tile(a["L1_gnn_b1"], 4)[:, None],
        "rw2": np.ascontiguousarray(a["L1_gnn_W2"].transpose(1, 0, 2).reshape(HID, NREL * NS)),
        "rr2": a["L1_gnn_root2"], "rb2": np.tile(a["L1_gnn_b2"], 8)[:, None], "cst16": c16, "cst32": c32,
    }
    nc = bacc.Bacc("TRN2", target_bir_lowering=False, num_devices=1)
    arrays = {f"in_{n}": np.ascontiguousarray(v) for n, v in arrays.items()}
    args = [nc.dram_tensor(n, v.shape, mybir.dt.from_np(v.dtype), kind="ExternalInput").ap() for n, v in arrays.items()]
    out = nc.dram_tensor("out", (NPAD, NS), mybir.dt.float32, kind="ExternalOutput").ap()
    gnn_kernel(nc, *args, out)
    r = run_bass_kernel_spmd(nc, [arrays], core_ids=[0])
    return np.ascontiguousarray(r.results[0]["out"][:NODES])
```

```python
import concourse.bass as bass
from concourse import mybir
from contextlib import ExitStack

NODES, EDGES = 3125, 103125
NS, NV, NREL, HID = 16, 4, 8, 32
FD = 3 * NS
EPS = 1e-5

P = 128
TILE_G = 4
GROUP = TILE_G * P
STEPS = -(-EDGES // (2 * GROUP))
GROUPS = 2 * STEPS
TILES = GROUPS * TILE_G
LO4, LO8, LO16 = 784, 392, 196
NPAD = 4 * LO4
CH = 98
C4, C8, C16 = LO4 // CH, LO8 // CH, LO16 // CH
NQ = NPAD // CH
Y1_EACH = 2 * C8
F1 = NS + 3 * NV + 1
M1 = 4 * F1
FT = NS + 3 * NV + NREL
RT = NV + FT
NW1 = (NS + NV) * NS
H1AT = 64
HROWS = FD + 1
PADS = NPAD - NODES
SEG_ACT = 2
LOW_ACT = 3
assert STEPS * 2 * GROUP >= EDGES and NODES < NPAD and PADS <= CH

K_IOTA, K_H29, K_H32, K_H16, K_END = 0, LO4, LO4 + M1, LO4 + M1 + P, LO4 + M1 + 2 * P
Q_ID, Q_CNT, Q_SUM, Q_SQ, Q_B0, Q_B1, Q_S16 = 0, P, P + M1, P + 2 * M1, P + 3 * M1, 2 * P + 3 * M1, 3 * P + 3 * M1
Q_PAD4 = 4 * P + 3 * M1
Q_ISS, Q_PAD8, Q_END = Q_PAD4 + 1, Q_PAD4 + 2, Q_PAD4 + 3


def gnn_kernel(nc, x, dst, src, typ, attr, vec, w1, fcb, w2a, w2b, bn0, bn1, rw1, rr1, rb1, rw2, rr2, rb2,
               cst16, cst32, out):
    f32, bf16, f16, i32, f32r = mybir.dt.float32, mybir.dt.bfloat16, mybir.dt.float16, mybir.dt.int32, mybir.dt.float32r
    ALU, ACT, AX = mybir.AluOpType, mybir.ActivationFunctionType, mybir.AxisListType.X
    ds = bass.ds

    hid_d = nc.dram_tensor("hid_d", (GROUPS, HROWS, GROUP), f32, kind="Internal").ap()
    row_d = nc.dram_tensor("row_d", (NPAD, FT), f32, kind="Internal").ap()
    cidx_d = nc.dram_tensor("cidx_d", (P, TILES), i32, kind="Internal").ap()
    y1_d = nc.dram_tensor("y1_d", (NPAD * NREL, HID), f32, kind="Internal").ap()
    y2_d = nc.dram_tensor("y2_d", (NPAD * NREL, NS), f32, kind="Internal").ap()

    ctx = ExitStack()
    with ctx:
        def sb(name, shape, dt=f32):
            return ctx.enter_context(nc.sbuf_tensor(name, shape, dt))

        def sem(name):
            return ctx.enter_context(nc.semaphore(name))

        def sems(name):
            return [sem(f"{name}{b}") for b in range(2)]

        k16, k32 = sb("k16", [P, K_END], f16), sb("k32", [P, Q_END])
        w1_s, fcb_s = sb("w1_s", [P, H1AT + HROWS]), sb("fcb_s", [H1AT + HROWS, 1])
        w2a_s, w2b_s = sb("w2a_s", [H1AT + HROWS, NW1]), sb("w2b_s", [H1AT + HROWS, NW1])
        bn0_s, bn1_s = sb("bn0_s", [M1, 2]), sb("bn1_s", [P, 2])
        rb1_s, rb2_s = sb("rb1_s", [P, 1]), sb("rb2_s", [P, 1])
        rw1_s = sb("rw1_s", [P, 8, NREL * HID])
        rr1_s = sb("rr1_s", [P, 2, 4, HID])
        rw2_s = sb("rw2_s", [P, 4, NREL * NS])
        rr2_s = sb("rr2_s", [P, 2, 8, NS])
        w2a_top, w2a_rest = sb("w2a_top", [H1AT + HROWS, NW1], f32r), sb("w2a_rest", [H1AT + HROWS, NW1], f32r)
        ysb = sb("ysb", [P, C8 * 8 * NREL * HID])
        src_i, dst_i, typ_i = (ysb[:, m * TILES:(m + 1) * TILES].bitcast(i32) for m in range(3))
        cidx_i = sb("cidx_i", [P, TILES], i32)
        typ_f = sb("typ_f", [P, TILES])
        s_hi4, s_lo4, s_hi8, s_lo8 = (sb(n, [P, TILES]) for n in ("s_hi4", "s_lo4", "s_hi8", "s_lo8"))
        d_hi4, d_lo4, d_hi8, d_lo8 = (sb(n, [P, TILES]) for n in ("d_hi4", "d_lo4", "d_hi8", "d_lo8"))
        d_lo16, d_seg, bit = sb("d_lo16", [P, TILES]), sb("d_seg", [P, TILES]), sb("bit", [P, TILES])
        early = sb("early", [P, TILES * NREL // 2])
        vec_s = early[:, 0:3 * TILES].rearrange("p (t c) -> p t c", c=3)
        tsel = early[:, :].bitcast(bf16).rearrange("p (t r) -> p t r", r=NREL)
        sh = sb("sh", [P, TILES, 3])
        norm = sb("norm", [P, TILES])
        we = sb("we", [P, TILES])
        ix = [sb(f"ix{b}", [P, TILE_G], i32) for b in range(2)]
        attr_s = [sb(f"attr{b}", [P, GROUP]) for b in range(2)]
        hid = [sb(f"hid{b}", [H1AT + HROWS, GROUP]) for b in range(2)]
        cut = [sb(f"cut{b}", [H1AT + HROWS, GROUP], f32r) for b in range(2)]
        rows = [sb(f"rows{b}", [P, TILE_G * RT]) for b in range(2)]
        low = [sb(f"low{b}", [P, TILE_G, LO4], bf16) for b in range(2)]
        high = [sb(f"high{b}", [P, TILE_G * P], bf16) for b in range(2)]
        dist = sb("dist", [P, TILE_G * P], bf16)
        ldist = sb("ldist", [P, LOW_ACT, LO8], bf16)
        ddist = sb("ddist", [P, TILE_G, LO16], bf16)
        sdist = sb("sdist", [P, SEG_ACT, P], bf16)
        dlow = [sb(f"dlow{b}", [P, TILE_G, LO16], bf16) for b in range(2)]
        dseg = [sb(f"dseg{b}", [P, TILE_G, P], bf16) for b in range(2)]
        stk = [sb(f"stk{b}", [P, 3, TILE_G * P], bf16) for b in range(2)]
        prod = sb("prod", [P, 2, 2 * NW1])
        msg = [sb(f"msg{b}", [P, TILE_G * (NV + F1)]) for b in range(2)]
        part = [sb(f"part{b}", [P, 3, TILE_G * HID], bf16) for b in range(2)]
        rest = sb("rest", [P, TILE_G * HID])
        uvec = sb("uvec", [P, TILE_G, NV, 3])
        tval = sb("tval", [P, TILE_G, NREL])
        acc = sb("acc", [P, LO4])
        rec = sb("rec", [P, LO4])
        sq = sb("sq", [P, LO4])
        zeros = sb("zeros", [P, LO8], bf16)
        cdt = sb("cdt", [P, LO16])
        st = sb("st", [P, 8])
        r2 = sb("r2", [CH, NQ, FT])
        xr = sb("xr", [CH, C8, 8 * NS])
        x1 = sb("x1", [CH, C8, 8 * NS])
        x2 = sb("x2", [CH, C8, 8 * NS])
        x1t = sb("x1t", [P, LO8])
        ht = sb("ht", [P, LO4])
        lnm, lnv, lnr = sb("lnm", [CH, NQ]), sb("lnv", [CH, NQ]), sb("lnr", [CH, NQ])
        lnd = sb("lnd", [CH, NQ, NS])

        PS = ctx.enter_context(nc.psum_tensor("PS", [P, 8, 512], f32))
        ACC, CNT, HP, WP = 0, 2, 3, 4

        s_small, s_edge, s_x = sem("small_loaded"), sem("edge_arrays_loaded"), sem("x_rows_loaded")
        s_blk, s_zero = sem("block_weights_loaded"), sem("cleared")
        s_ix = [sems(f"index_loaded{n}_") for n in range(4)]
        s_gat = [sems(f"rows_gathered{n}_") for n in range(4)]
        s_in = [sems(f"net_input_loaded{n}_") for n in range(2)]
        s_hid, s_relu, s_hst = sem("hidden_made"), sem("hidden_rectified"), sems("hidden_stored")
        s_cut, s_wcut = sem("hidden_rest_left"), sem("weights_cut")
        s_w = [sem(f"weights_made{n}") for n in range(2)]
        s_prod = [sem(f"products_made{n}") for n in range(2)]
        s_red = [sem(f"messages_made{n}") for n in range(4)]
        s_cast0 = [sem(f"first_part_cut{n}") for n in range(4)]
        s_cast1 = [sem(f"second_part_cut{n}") for n in range(4)]
        s_sub = [sem(f"rest_left{n}") for n in range(4)]
        s_mask = [sem(f"hi_onehot{n}") for n in range(4)]
        s_stk = [sem(f"stack_ready{n}") for n in range(4)]
        s_scat = [sem(f"group_summed{n}") for n in range(4)]
        s_u, s_t = sem("vector_products"), sem("relation_weight")
        s_pre, s_sqrt, s_rt = sem("edge_arrays_made"), sem("norm_squared"), sem("norm_rooted")
        s_edge_made, s_cidx, s_node, s_pe, s_act = sem("per_edge_ready"), sem("cidx_stored"), sem("node_step"), sem("node_product"), sem("node_root")
        s_tab, s_ysb, s_out = sem("table_stored"), sem("table_rows_made"), sem("out_stored")
        s_go = sem("gather_may_start")
        s_late, s_yact, s_rest = sem("late_loaded"), sem("odd_table_rows_made"), sem("second_pass_arrays")
        s_clear, s_dif, s_hold = sem("operands_cleared"), [sem(f"distances_made{n}") for n in range(4)], sem("scalar_may_go")

        def k(col, n, rows_=P):
            return k32[0:rows_, col:col + n]

        HIGH = [(M1, K_H29, s_hi4), (P, K_H16, s_hi8), (P, K_H32, d_hi4), (P, K_H16, d_hi8)]
        LOW = [(s_lo4, LO4), (s_lo8, LO8), (d_lo4, LO4), (d_lo8, LO8)]
        MESSAGE = [F1, NS, HID, NS]
        REDUCTIONS = [3, 1, 1, 1]

        def message(n, b):
            f, before = MESSAGE[n], NV if n == 0 else 0
            return msg[b][:, 0:TILE_G * (before + f)].rearrange("p (t f) -> p t f", f=before + f)[:, :, before:]

        def parts(n, b, m):
            return part[b][:, m, 0:TILE_G * MESSAGE[n]].rearrange("p (t f) -> p t f", f=MESSAGE[n])

        def rests(n):
            return rest[:, 0:TILE_G * MESSAGE[n]].rearrange("p (t f) -> p t f", f=MESSAGE[n])

        def groups(eng, step):
            step(0, 0)
            step(1, 1)
            with eng.Fori(1, STEPS) as i:
                step(2 * i, 0)
                step(2 * i + 1, 1)

        def pipelined(eng, step):
            step(0, 0)
            step(1, 1)
            with eng.Fori(1, STEPS - 1) as i:
                step(2 * i, 0)
                step(2 * i + 1, 1)
            step(GROUPS - 2, 0)
            step(GROUPS - 1, 1)

        def first(g, n=2):
            return isinstance(g, int) and g < n

        def last_group(g):
            return isinstance(g, int) and g == GROUPS - 1

        def turn(g, b):
            return g // 2 + 1 if isinstance(g, int) else (g - b) // 2 + 1

        block = ctx.enter_context(nc.Block())

        @block.sync
        def _(eng):
            eng.dma_start(vec_s, vec).then_inc(s_edge, 16)
            for t, s in ((typ_i, typ), (src_i, src), (dst_i, dst)):
                eng.dma_start(t[:, :], s).then_inc(s_edge, 16)
            eng.wait_ge(s_clear, 1)
            for t, s in ((k16, cst16), (w1_s[0:FD], w1), (fcb_s, fcb), (w2a_s[0:HROWS], w2a),
                         (w2a_s[H1AT:H1AT + HROWS], w2a), (w2b_s[H1AT:H1AT + HROWS], w2b)):
                eng.dma_start(t[:, :], s).then_inc(s_small, 16)

            def load_late():
                for t, s in ((k32, cst32), (bn0_s, bn0), (bn1_s, bn1), (rb1_s, rb1), (rb2_s, rb2)):
                    eng.dma_start(t[:, :], s).then_inc(s_late, 16)
                xv = x.rearrange("(h c p) f -> c p h f", c=C8, p=CH)
                for c in range(C8):
                    eng.dma_start(xr[:, c, :].rearrange("p (h f) -> p h f", h=8), xv[c]).then_inc(s_x, 16)
                eng.wait_ge(s_zero, 1)
                for h in range(8):
                    eng.dma_start(rw1_s[h * NS:(h + 1) * NS, h, :], rw1).then_inc(s_blk, 16)
                    eng.dma_start(rr1_s[h * NS:(h + 1) * NS, h % 2, h // 2, :], rr1).then_inc(s_blk, 16)
                    eng.dma_start(rr2_s[(h // 2) * HID:(h // 2 + 1) * HID, h % 2, h, :], rr2).then_inc(s_blk, 16)
                for h in range(4):
                    eng.dma_start(rw2_s[h * HID:(h + 1) * HID, h, :], rw2).then_inc(s_blk, 16)

            def load_ix(n, g, b, idx):
                if not first(g):
                    eng.wait_ge(s_gat[n][b], (turn(g, b) - 1) * (16 * TILE_G))
                at = ds(g * TILE_G, TILE_G) if not isinstance(g, int) else slice(g * TILE_G, (g + 1) * TILE_G)
                eng.dma_start(ix[b][:, :], idx[:, at]).then_inc(s_ix[n][b], 16)

            def pass1(g, b):
                load_ix(0, g, b, dst)
                if not first(g):
                    eng.wait_ge(s_hid, g - 1)
                at = ds(g * GROUP, GROUP) if not isinstance(g, int) else slice(g * GROUP, (g + 1) * GROUP)
                eng.dma_start(attr_s[b][0:FD, :], attr[:, at]).then_inc(s_in[0][b], 16)
            groups(eng, pass1)
            load_late()

            for b in range(2):
                eng.wait_ge(s_hst[b], 16 * STEPS)
                eng.wait_ge(s_gat[0][b], 16 * TILE_G * STEPS)

            def pass2(g, b):
                load_ix(1, g, b, dst)
                if not first(g):
                    eng.wait_ge(s_w[1], 2 * (g - 1))
                at = ds(g, 1) if not isinstance(g, int) else slice(g, g + 1)
                eng.dma_start(hid[b][H1AT:H1AT + HROWS, :], hid_d[at, :, :].rearrange("a k n -> k (a n)")).then_inc(s_in[1][b], 16)
            eng.wait_ge(s_w[0], 2 * GROUPS)
            groups(eng, pass2)

            eng.wait_ge(s_pre, 1)
            eng.dma_start(cidx_d, cidx_i[:, :]).then_inc(s_cidx, 16)
            eng.wait_ge(s_cidx, 16)
            for b in range(2):
                eng.wait_ge(s_gat[1][b], 16 * TILE_G * STEPS)
            yd = y1_d.rearrange("(h c p r) f -> c p h (r f)", h=8, c=C8, p=CH)
            for c in range(C8):
                eng.wait_ge(s_ysb, 2 * (c + 1))
                eng.wait_ge(s_yact, 2 * (c + 1))
                eng.dma_start(yd[c], ysb[0:CH, c * 8 * NREL * HID:(c + 1) * 8 * NREL * HID]
                              .rearrange("p (h r) -> p h r", h=8)).then_inc(s_tab, 16)
            groups(eng, lambda g, b: load_ix(2, g, b, cidx_d))
            for b in range(2):
                eng.wait_ge(s_gat[2][b], 16 * TILE_G * STEPS)
            yd = y2_d.rearrange("(h c p r) f -> c p h (r f)", h=4, c=C4, p=CH)
            for c in range(C4):
                even, odd = Y1_EACH + c // 2 + 1, Y1_EACH + (c + 1) // 2
                eng.wait_ge(s_ysb, even)
                eng.wait_ge(s_yact, odd)
                eng.dma_start(yd[c], ysb[0:CH, c * 512:(c + 1) * 512].rearrange("p (h r) -> p h r", h=4))\
                   .then_inc(s_tab, 16)
            groups(eng, lambda g, b: load_ix(3, g, b, cidx_d))

            eng.wait_ge(s_node, NODE_OUT)
            ov = out.rearrange("(h c p) f -> c p h f", c=C8, p=CH)
            for c in range(C8):
                eng.dma_start(ov[c], x2[:, c, :].rearrange("p (h f) -> p h f", h=8)).then_inc(s_out, 16)
            eng.wait_ge(s_out, 16 * C8)

        @block.gpsimd
        def _(eng):
            for t in (cut[0], cut[1]):
                eng.memset(t[:, :].bitcast(f32), 0.0)
            for t in (w1_s, w2a_s, w2b_s, attr_s[0], attr_s[1]):
                last = eng.memset(t[:, :], 0.0)
            last.then_inc(s_clear, 1)
            for t in (rw1_s, rw2_s):
                eng.memset(t[:, :, :], 0.0)
            for t in (rr1_s, rr2_s):
                last = eng.memset(t[:, :, :, :], 0.0)
            last.then_inc(s_zero, 1)
            eng.wait_ge(s_zero, 1)

            def gather(n, g, b, table, width, used, room=0):
                eng.wait_ge(s_ix[n][b], 16 * turn(g, b))
                if not first(g):
                    used(g)
                eng.sem_inc(s_go, 1)
                for u in range(TILE_G):
                    eng.indirect_dma_start(rows[b][:, u * (width + room) + room:(u + 1) * (width + room)], None, table,
                                           bass.IndirectOffsetOnAxis(ix[b][:, u:u + 1], 0)).then_inc(s_gat[n][b], 16)

            def pass1(g, b):
                gather(0, g, b, x, NS, lambda g: eng.wait_ge(s_prod[0], 2 * (g - 1)))
                eng.wait_ge(s_relu, g + 1)
                nc.gpsimd.tensor_tensor(cut[b][H1AT:H1AT + HROWS, :], hid[b][0:HROWS, :], cut[b][0:HROWS, :].bitcast(f32),
                                        ALU.subtract).then_inc(s_cut, 1)
            groups(eng, pass1)
            eng.wait_ge(s_prod[0], 2 * GROUPS)
            eng.wait_ge(s_tab, 16)

            groups(eng, lambda g, b: gather(1, g, b, row_d, FT, lambda g: eng.wait_ge(s_prod[1], 2 * (g - 1)), NV))
            eng.wait_ge(s_prod[1], 2 * GROUPS)
            eng.wait_ge(s_tab, 16 * (1 + C8))
            groups(eng, lambda g, b: gather(2, g, b, y1_d, HID, lambda g: eng.wait_ge(s_red[2], g - 1)))
            eng.wait_ge(s_red[2], GROUPS)
            eng.wait_ge(s_tab, 16 * (1 + C8 + C4))
            groups(eng, lambda g, b: gather(3, g, b, y2_d, NS, lambda g: eng.wait_ge(s_red[3], g - 1)))

        @block.tensor
        def _(eng):
            mm = nc.tensor.matmul
            eng.wait_ge(s_small, 96)

            def scatter(n, g, b, cols, lo, halves):
                eng.wait_ge(s_stk[n], g + 1)
                for u in range(TILE_G):
                    for part_ in range(3):
                        for half in range(halves):
                            last = mm(PS[0:cols, ACC + half, 0:LO8], stk[b][:, part_, u * cols:(u + 1) * cols],
                                      low[b][:, u, half * LO8:(half + 1) * LO8], start=False, stop=True,
                                      skip_group_check=True)
                    if n == 0:
                        last = mm(PS[:, CNT, 0:LO16], dseg[b][:, u, :], dlow[b][:, u, :], start=False, stop=True,
                                  skip_group_check=True)
                last.then_inc(s_scat[n], 1)

            def make_hidden(g, b):
                eng.wait_ge(s_in[0][b], 16 * turn(g, b))
                if not first(g, 1):
                    eng.wait_ge(s_relu, g)
                mm(PS[0:H1AT + HROWS, HP, :], w1_s[:, :], attr_s[b][:, :], start=True, stop=True).then_inc(s_hid, 1)

            def make_weights(n, g, rows_, weights):
                for h in range(2):
                    if not first(g, 1):
                        eng.wait_ge(s_prod[n], 2 * g - 1 + h)
                    for u in range(2):
                        for m, w2 in enumerate(weights):
                            last = mm(PS[:, WP + 2 * h + u, 0:NW1], rows_[:, (2 * h + u) * P:(2 * h + u + 1) * P],
                                      w2, start=m == 0, stop=m == len(weights) - 1)
                    last.then_inc(s_w[n], 1)

            def step1(g, b):
                eng.wait_ge(s_cut, g + 1)
                make_weights(0, g, cut[b], [w2a_top[:, :], w2a_rest[:, :]])
                if not (isinstance(g, int) and g >= GROUPS - 2):
                    make_hidden(g + 2, b)
                if not first(g):
                    scatter(0, g - 2, b, M1, LO4, 2)

            eng.wait_ge(s_node, 1)
            for half in range(2):
                mm(PS[:, ACC + half, 0:LO8], zeros[:, 0:P], zeros[:, 0:LO8], start=True, stop=True, skip_group_check=True)
            mm(PS[:, CNT, 0:LO16], zeros[:, 0:P], zeros[:, 0:LO16], start=True, stop=True, skip_group_check=True)\
                .then_inc(s_scat[0], 1)
            make_hidden(0, 0)
            make_hidden(1, 1)
            eng.wait_ge(s_wcut, 1)
            pipelined(eng, step1)
            for g in (GROUPS - 2, GROUPS - 1):
                scatter(0, g, g % 2, M1, LO4, 2)

            pe = [0]

            def done(ins):
                pe[0] += 1
                ins.then_inc(s_pe, 1)

            eng.wait_ge(s_late, 80)
            eng.wait_ge(s_node, 3)
            for half in range(2):
                last = mm(PS[0:M1, HP + half, 0:LO8], k(Q_CNT, M1, M1), acc[0:M1, half * LO8:(half + 1) * LO8],
                          start=True, stop=True)
            done(last)
            eng.wait_ge(s_node, NODE_SUM1)
            done(mm(PS[0:M1, 5, 0:1], k(Q_SUM, M1, M1), st[0:M1, 0:1], start=True, stop=True))
            eng.wait_ge(s_node, NODE_SQ1)
            done(mm(PS[0:M1, 6, 0:1], k(Q_SQ, M1, M1), st[0:M1, 2:3], start=True, stop=True))
            for half in range(2):
                last = mm(PS[:, 7, 0:LO8], k(Q_B0 + half * P, P, M1), rec[0:M1, half * LO8:(half + 1) * LO8],
                          start=half == 0, stop=half == 1)
            done(last)
            eng.wait_ge(s_node, NODE_BN1)
            for c in range(C4):
                last = nc.tensor.transpose(PS[0:CH, c // 4, (c % 4) * M1:(c % 4 + 1) * M1],
                                           acc[0:M1, c * CH:(c + 1) * CH], k(Q_ID, M1, M1))
            for c in range(C16):
                last = nc.tensor.transpose(PS[0:CH, 2, c * P:(c + 1) * P], cdt[:, c * CH:(c + 1) * CH], k(Q_ID, P))
            done(last)

            eng.wait_ge(s_node, NODE_ROWS1)
            mm(PS[:, ACC, 0:LO8], zeros[:, 0:P], zeros[:, 0:LO8], start=True, stop=True, skip_group_check=True)\
                .then_inc(s_scat[1], 1)

            def step2(g, b):
                eng.wait_ge(s_in[1][b], 16 * turn(g, b))
                make_weights(1, g, hid[b], [w2b_s[:, :]])
                if not first(g):
                    scatter(1, g - 2, b, P, LO8, 1)
            groups(eng, step2)
            for g in (GROUPS - 2, GROUPS - 1):
                scatter(1, g, g % 2, P, LO8, 1)

            eng.wait_ge(s_node, NODE_SUM2)
            done(mm(PS[:, 5, 0:1], k(Q_S16, P), st[:, 0:1], start=True, stop=True))
            eng.wait_ge(s_node, NODE_SQ2)
            done(mm(PS[:, 6, 0:1], k(Q_S16, P), st[:, 2:3], start=True, stop=True))
            eng.wait_ge(s_node, NODE_BN2)
            for c in range(C8):
                last = nc.tensor.transpose(PS[0:CH, 2, c * P:(c + 1) * P], acc[:, c * CH:(c + 1) * CH], k(Q_ID, P))
            done(last)
            eng.wait_ge(s_node, NODE_X1)
            for c in range(C8):
                last = nc.tensor.transpose(PS[:, 3, c * CH:(c + 1) * CH], x1[:, c, :], k(Q_ID, CH, CH))
            done(last)
            eng.wait_ge(s_node, NODE_X1T)
            eng.wait_ge(s_blk, 16 * 28)
            for n in range(4 * C8):
                if n >= 4:
                    eng.wait_ge(s_yact if n % 2 else s_ysb, n // 2 - 1)
                done(mm(PS[0:CH, 4 + n % 4, :], x1t[:, (n // 4) * CH:(n // 4 + 1) * CH],
                        rw1_s[:, 2 * (n % 4):2 * (n % 4) + 2, :].rearrange("p h r -> p (h r)"), start=True, stop=True))
            for half in range(2):
                last = mm(PS[:, ACC + half, 0:LO8], rr1_s[:, half, :, :].rearrange("p h f -> p (h f)"), x1t[:, :],
                          start=True, stop=True, skip_group_check=True)
            last.then_inc(s_scat[2], 1)
            groups(eng, lambda g, b: scatter(2, g, b, P, LO4, 2))

            eng.wait_ge(s_act, ACT_H)
            for n in range(C4):
                eng.wait_ge(s_yact if n % 2 else s_ysb, Y1_EACH + n // 2 - 1)
                done(mm(PS[0:CH, 4 + n % 4, :], ht[:, n * CH:(n + 1) * CH], rw2_s[:, :, :].rearrange("p h r -> p (h r)"),
                        start=True, stop=True))
            for half in range(2):
                last = mm(PS[:, 2, 0:LO8], rr2_s[:, half, :, :].rearrange("p h f -> p (h f)"),
                          ht[:, half * LO8:(half + 1) * LO8], start=half == 0, stop=half == 1, skip_group_check=True)
            last.then_inc(s_scat[3], 1)

            def scatter4(g, b):
                eng.wait_ge(s_stk[3], g + 1)
                for u in range(TILE_G):
                    for part_ in range(3):
                        last = mm(PS[:, 2, 0:LO8], stk[b][:, part_, u * P:(u + 1) * P], low[b][:, u, 0:LO8],
                                  start=False, stop=True, skip_group_check=True)
                last.then_inc(s_scat[3], 1)
            groups(eng, scatter4)
            eng.wait_ge(s_node, NODE_B2)
            for c in range(C8):
                last = nc.tensor.transpose(PS[0:CH, 3, c * P:(c + 1) * P], acc[:, c * CH:(c + 1) * CH], k(Q_ID, P))
            done(last)
            assert pe[0] == PE_OUT

        @block.scalar
        def _(eng):
            act = nc.scalar.activation
            shf = sh[:, :, :].rearrange("p t c -> p (t c)")
            eng.wait_ge(s_edge, 64)
            act(shf, early[:, 0:3 * TILES], ACT.Square).then_inc(s_rt, 1)
            eng.wait_ge(s_sqrt, 2)
            act(norm[:, :], norm[:, :], ACT.Sqrt).then_inc(s_rt, 1)
            eng.wait_ge(s_small, 96)

            def tile(g, u):
                return ds(g * TILE_G + u, 1) if not isinstance(g, int) else slice(g * TILE_G + u, g * TILE_G + u + 1)

            def distances(n, g):
                cols, kcol, hi = HIGH[n]
                if not first(g, 1):
                    eng.wait_ge(s_mask[n], g)
                eng.sem_inc(s_hold, 1)
                for u in range(TILE_G):
                    last = act(dist[:, u * cols:(u + 1) * cols], k16[:, kcol:kcol + cols], ACT.Abs,
                               bias=hi[:, tile(g, u)], scale=-1.0)
                    if n == 0:
                        last = act(ddist[:, u, :], k16[:, K_IOTA:K_IOTA + LO16], ACT.Abs,
                                   bias=d_lo16[:, tile(g, u)], scale=-1.0)
                    if n == 0 and u < SEG_ACT:
                        last = act(sdist[:, u, :], k16[:, K_IOTA:K_IOTA + P], ACT.Abs,
                                   bias=d_seg[:, tile(g, u)], scale=-1.0)
                    if n == 1 and u < LOW_ACT:
                        last = act(ldist[:, u, :], k16[:, K_IOTA:K_IOTA + LO8], ACT.Abs,
                                   bias=s_lo8[:, tile(g, u)], scale=-1.0)
                last.then_inc(s_dif[n], 1)

            def masks(n, g, b):
                cols = HIGH[n][0]
                if not first(g):
                    eng.wait_ge(s_scat[n], g)
                eng.wait_ge(s_dif[n], g + 1)
                if n == 0:
                    act(dlow[b][:, :, :], ddist[:, :, :], ACT.Relu, bias=1.0, scale=-1.0)
                    act(dseg[b][:, 0:SEG_ACT, :], sdist[:, :, :], ACT.Relu, bias=1.0, scale=-1.0)
                if n == 1:
                    act(low[b][:, 0:LOW_ACT, 0:LO8], ldist[:, :, :], ACT.Relu, bias=1.0, scale=-1.0)
                act(high[b][:, 0:TILE_G * cols], dist[:, 0:TILE_G * cols], ACT.Relu, bias=1.0, scale=-1.0)\
                    .then_inc(s_mask[n], 1)

            def casts_and_masks(n, g, b):
                w = TILE_G * MESSAGE[n]
                eng.wait_ge(s_red[n], (g + 1) * REDUCTIONS[n])
                act(parts(n, b, 0), message(n, b), ACT.Copy).then_inc(s_cast0[n], 1)
                masks(n, g, b)
                eng.wait_ge(s_sub[n], 2 * g + 1)
                act(part[b][:, 1, 0:w], rest[:, 0:w], ACT.Copy).then_inc(s_cast1[n], 1)

            def behind(n, g, b):
                if not first(g, 1):
                    casts_and_masks(n, g - 1, 1 - b)

            def finish(n):
                casts_and_masks(n, GROUPS - 1, 1)

            eng.wait_ge(s_edge_made, 1)
            act(shf, shf, ACT.Copy, scale=3.0 ** 0.5).then_inc(s_rt, 1)

            def rectify(g, b):
                eng.wait_ge(s_hid, g + 1)
                if not first(g):
                    eng.wait_ge(s_cut, g - 1)
                    eng.wait_ge(s_hst[b], 16 * (turn(g, b) - 1))
                    eng.wait_ge(s_w[0], 2 * (g - 1))
                act(cut[b][0:HROWS, :], PS[0:HROWS, HP, :], ACT.Relu, bias=fcb_s[0:HROWS, 0:1])
                act(hid[b][:, :], PS[0:H1AT + HROWS, HP, :], ACT.Relu, bias=fcb_s[:, 0:1]).then_inc(s_relu, 1)

            def store_hidden(g, b):
                eng.wait_ge(s_relu, g + 1)
                at = ds(g, 1) if not isinstance(g, int) else slice(g, g + 1)
                eng.dma_start(hid_d[at, :, :].rearrange("a k n -> k (a n)"), hid[b][H1AT:H1AT + HROWS, :])\
                   .then_inc(s_hst[b], 16)

            def pass1(g, b):
                behind(0, g, b)
                ends = isinstance(g, int) and g >= GROUPS - 2
                if not ends:
                    rectify(g + 2, b)
                distances(0, g)
                if not ends:
                    store_hidden(g + 2, b)
            for b in range(2):
                rectify(b, b)
                store_hidden(b, b)
            pipelined(eng, pass1)
            finish(0)

            def root(n, value):
                eng.wait_ge(s_node, value)
                act(st[0:n, 3:4], st[0:n, 3:4], ACT.Sqrt).then_inc(s_act, 1)
            root(M1, NODE_VAR1)
            act(shf, shf, ACT.Copy, scale=3.0 ** -0.5).then_inc(s_rt, 1)
            eng.wait_ge(s_node, NODE_ROWS1)
            eng.dma_start(row_d.rearrange("(q p) f -> p q f", p=CH), r2[:, :, :]).then_inc(s_tab, 16)

            def pass2(g, b):
                behind(1, g, b)
                distances(1, g)
            eng.wait_ge(s_rest, 1)
            pipelined(eng, pass2)
            finish(1)
            root(P, NODE_VAR2)
            eng.wait_ge(s_node, NODE_LN1)
            act(lnr[:, :], lnv[:, :], ACT.Sqrt).then_inc(s_act, 1)
            y1v = ysb[0:CH, :].rearrange("p (n m) -> p n m", m=512)

            def odd_rows(count, before):
                for n in range(1, count, 2):
                    eng.wait_ge(s_pe, before + n + 1)
                    act(y1v[:, n, :], PS[0:CH, 4 + n % 4, :], ACT.Copy).then_inc(s_yact, 1)
            odd_rows(4 * C8, 9)

            def relational(n):
                def step(g, b):
                    behind(n, g, b)
                    distances(n, g)
                pipelined(eng, step)
                finish(n)
            relational(2)
            eng.wait_ge(s_scat[2], 1 + GROUPS)
            for half in range(2):
                last = act(ht[:, half * LO8:(half + 1) * LO8], PS[:, ACC + half, 0:LO8], ACT.Relu, bias=rb1_s[:, 0:1])
            last.then_inc(s_act, 1)
            eng.wait_ge(s_tab, 16 * (1 + C8))
            odd_rows(C4, 9 + 4 * C8)
            relational(3)
            eng.wait_ge(s_node, NODE_LN2)
            act(lnr[:, :], lnv[:, :], ACT.Sqrt).then_inc(s_act, 1)
            eng.wait_ge(s_tab, 16 * (1 + C8 + C4))

        @block.vector
        def _(eng):
            v = nc.vector
            node = [0]

            def link(ins):
                node[0] += 1
                ins.then_inc(s_node, 1)
                eng.wait_ge(s_node, node[0])

            def at(name, value):
                assert node[0] == value, (name, node[0])

            link(v.memset(zeros[:, :], 0.0))
            for b in range(2):
                last = v.memset(msg[b][:, :], 1.0)
            link(last)
            eng.wait_ge(s_edge, 64)
            chain = [0]

            def step(ins):
                chain[0] += 1
                ins.then_inc(s_sqrt, 1)
                eng.wait_ge(s_sqrt, chain[0])

            step(v.tensor_copy(typ_f[:, :], typ_i[:, :]))
            eng.wait_ge(s_rt, 1)
            step(v.tensor_reduce(norm[:, :], sh[:, :, :], AX, ALU.add))
            def split4(i, hi4, lo4):
                step(v.tensor_copy(lo4[:, :], i[:, :]))
                step(v.tensor_scalar(hi4[:, :], lo4[:, :], float(LO4), None, ALU.is_ge))
                for m in (2, 3):
                    step(v.scalar_tensor_tensor(hi4[:, :], lo4[:, :], float(m * LO4), hi4[:, :], ALU.is_ge, ALU.add))
                step(v.scalar_tensor_tensor(lo4[:, :], hi4[:, :], -float(LO4), lo4[:, :], ALU.mult, ALU.add))

            def split8(hi4, lo4, hi8, lo8):
                step(v.tensor_scalar(bit[:, :], lo4[:, :], float(LO8), None, ALU.is_ge))
                step(v.scalar_tensor_tensor(hi8[:, :], hi4[:, :], 2.0, bit[:, :], ALU.mult, ALU.add))
                step(v.scalar_tensor_tensor(lo8[:, :], bit[:, :], -float(LO8), lo4[:, :], ALU.mult, ALU.add))
            split4(src_i, s_hi4, s_lo4)
            eng.wait_ge(s_rt, 2)
            step(v.tensor_scalar(norm[:, :], norm[:, :], 1e-12, None, ALU.add))
            step(v.reciprocal(norm[:, :], norm[:, :]))
            step(v.tensor_tensor(sh[:, :, :], vec_s, norm[:, :].unsqueeze(2).broadcast_to([P, TILES, 3]), ALU.mult))
            split4(dst_i, d_hi4, d_lo4)
            split8(d_hi4, d_lo4, d_hi8, d_lo8)
            step(v.tensor_scalar(bit[:, :], d_lo8[:, :], float(LO16), None, ALU.is_ge))
            step(v.scalar_tensor_tensor(d_lo16[:, :], bit[:, :], -float(LO16), d_lo8[:, :], ALU.mult, ALU.add))
            step(v.scalar_tensor_tensor(d_seg[:, :], d_hi8[:, :], 2.0, bit[:, :], ALU.mult, ALU.add))
            v.scalar_tensor_tensor(d_seg[:, :], d_seg[:, :], float(NREL), typ_f[:, :], ALU.mult, ALU.add)\
             .then_inc(s_edge_made, 1)
            eng.wait_ge(s_edge_made, 1)

            def later_arrays():
                split8(s_hi4, s_lo4, s_hi8, s_lo8)
                v.tensor_tensor(tsel, k16[:, K_IOTA:K_IOTA + NREL].unsqueeze(1).broadcast_to([P, TILES, NREL]),
                                typ_f[:, :].unsqueeze(2).broadcast_to([P, TILES, NREL]), ALU.is_equal)\
                 .then_inc(s_rest, 1)
                step(v.tensor_copy(bit[:, :], src_i[:, :]))
                step(v.scalar_tensor_tensor(bit[:, :], bit[:, :], float(NREL), typ_f[:, :], ALU.mult, ALU.add))
                v.tensor_copy(cidx_i[:, :], bit[:, :]).then_inc(s_pre, 1)
                eng.wait_ge(s_rest, 1)

            eng.wait_ge(s_small, 96)
            eng.wait_ge(s_rt, 3)

            def tile(g, u):
                return ds(g * TILE_G + u, 1) if not isinstance(g, int) else slice(g * TILE_G + u, g * TILE_G + u + 1)

            def tiles(g):
                return ds(g * TILE_G, TILE_G) if not isinstance(g, int) else slice(g * TILE_G, (g + 1) * TILE_G)

            def first_rest(n, g, b):
                eng.wait_ge(s_cast0[n], g + 1)
                v.tensor_tensor(rests(n), message(n, b), parts(n, b, 0), ALU.subtract).then_inc(s_sub[n], 1)

            def second_rest(n, g, b):
                if not first(g):
                    eng.wait_ge(s_scat[n], g)
                lo, width = LOW[n]
                for u in range(TILE_G):
                    if n == 0 and u >= SEG_ACT:
                        v.tensor_scalar(dseg[b][:, u, :], k16[:, K_IOTA:K_IOTA + P], d_seg[:, tile(g, u)], None,
                                        ALU.is_equal)
                    if n != 1 or u >= LOW_ACT:
                        v.tensor_scalar(low[b][:, u, 0:width], k16[:, K_IOTA:K_IOTA + width], lo[:, tile(g, u)], None,
                                        ALU.is_equal)
                w = TILE_G * MESSAGE[n]
                eng.wait_ge(s_cast1[n], g + 1)
                v.tensor_tensor(part[b][:, 2, 0:w], rest[:, 0:w], part[b][:, 1, 0:w], ALU.subtract).then_inc(s_sub[n], 1)

            def stack(n, g, b, parts_=range(3)):
                f, w = MESSAGE[n], TILE_G * MESSAGE[n]
                a = HIGH[n][0] // f
                if 0 in parts_:
                    eng.wait_ge(s_mask[n], g + 1)
                    eng.wait_ge(s_sub[n], 2 * g + 2)
                for m in parts_:
                    last = v.tensor_tensor(
                        stk[b][:, m, 0:w * a].rearrange("p (t h f) -> p t h f", h=a, f=f),
                        high[b][:, 0:w * a].rearrange("p (t h f) -> p t h f", h=a, f=f),
                        part[b][:, m, 0:w].rearrange("p (t f) -> p t f", f=f).unsqueeze(2).broadcast_to([P, TILE_G, a, f]),
                        ALU.mult)
                if 2 in parts_:
                    last.then_inc(s_stk[n], 1)

            def finish(n):
                first_rest(n, GROUPS - 1, 1)
                second_rest(n, GROUPS - 1, 1)
                stack(n, GROUPS - 1, 1)

            def products(n, g, h, x_in, nj, ni):
                eng.wait_ge(s_w[n], 2 * g + 1 + h)
                v.tensor_tensor(prod[:, h, :].rearrange("p (t j i) -> p t j i", t=2, j=nj),
                                PS[:, WP + 2 * h:WP + 2 * h + 2, 0:NW1].rearrange("p t (j i) -> p t j i", j=nj),
                                x_in[:, 2 * h:2 * h + 2, :].unsqueeze(2).broadcast_to([P, 2, nj, ni]),
                                ALU.mult).then_inc(s_prod[n], 1)

            def pass1(g, b):
                if not first(g, 1):
                    first_rest(0, g - 1, 1 - b)
                eng.wait_ge(s_gat[0][b], 16 * TILE_G * turn(g, b))
                xg = rows[b][:, 0:TILE_G * NS].rearrange("p (t f) -> p t f", f=NS)
                mv = msg[b][:, :].rearrange("p (t f) -> p t f", f=NV + F1)
                for h in range(2):
                    products(0, g, h, xg, NV + NS, NS)
                if not first(g, 1):
                    second_rest(0, g - 1, 1 - b)
                for h in range(2):
                    eng.wait_ge(s_prod[0], 2 * g + 1 + h)
                    pv = prod[:, h, :].rearrange("p (t j i) -> p t j i", t=2, j=NV + NS)
                    v.tensor_reduce(mv[:, 2 * h:2 * h + 2, 0:NV + NS], pv, AX, ALU.add).then_inc(s_red[0], 1)
                if not first(g, 1):
                    stack(0, g - 1, 1 - b, [0])
                eng.wait_ge(s_red[0], 3 * g + 2)
                v.tensor_tensor(mv[:, :, NV + NS:NV + NS + 3 * NV].rearrange("p t (j c) -> p t j c", c=3),
                                mv[:, :, 0:NV].unsqueeze(3).broadcast_to([P, TILE_G, NV, 3]),
                                sh[:, tiles(g), :].unsqueeze(2).broadcast_to([P, TILE_G, NV, 3]),
                                ALU.mult).then_inc(s_red[0], 1)
                if not first(g, 1):
                    stack(0, g - 1, 1 - b, [1, 2])
            step(v.tensor_copy(w2a_top[:, :], w2a_s[:, :]))
            v.tensor_tensor(w2a_rest[:, :], w2a_s[:, :], w2a_top[:, :].bitcast(f32), ALU.subtract).then_inc(s_wcut, 1)
            groups(eng, pass1)
            finish(0)

            at("start", 2)
            eng.wait_ge(s_scat[0], 1 + GROUPS)
            link(v.tensor_copy(acc[0:M1, :].rearrange("p (a n) -> p a n", a=2), PS[0:M1, ACC:ACC + 2, 0:LO8]))
            eng.wait_ge(s_pe, 1)
            link(v.tensor_scalar(rec[0:M1, :].rearrange("p (a n) -> p a n", a=2), PS[0:M1, HP:HP + 2, 0:LO8], 1.0, None,
                                 ALU.max))
            link(v.reciprocal(rec[0:M1, :], rec[0:M1, :]))
            link(v.scalar_tensor_tensor(acc[0:M1, :], acc[0:M1, :], NS ** -0.5, rec[0:M1, :], ALU.mult, ALU.mult))

            def batch_norm(n, width, bank_sum, pe_sum, pad_col, only, bn, n_act):
                def clear_pads():
                    link(v.tensor_scalar(acc[0:n, width - PADS:width], acc[0:n, width - PADS:width],
                                         k(pad_col, 1, n), None, ALU.mult))
                clear_pads()
                link(v.tensor_reduce(st[0:n, 0:1], acc[0:n, 0:width], AX, ALU.add))
                yield
                eng.wait_ge(s_pe, pe_sum)
                if only is None:
                    link(v.tensor_scalar(st[0:n, 1:2], PS[0:n, 5, 0:1], 1.0 / NODES, None, ALU.mult))
                else:
                    link(v.tensor_scalar(st[0:n, 1:2], PS[0:n, 5, 0:1], k(only, 1, n), 1.0 / NODES, ALU.mult, ALU.mult))
                link(v.tensor_scalar(acc[0:n, 0:width], acc[0:n, 0:width], st[0:n, 1:2], None, ALU.subtract))
                clear_pads()
                link(v.tensor_tensor(sq[0:n, 0:width], acc[0:n, 0:width], acc[0:n, 0:width], ALU.mult))
                link(v.tensor_reduce(st[0:n, 2:3], sq[0:n, 0:width], AX, ALU.add))
                yield
                eng.wait_ge(s_pe, pe_sum + 1)
                link(v.tensor_scalar(st[0:n, 3:4], PS[0:n, 6, 0:1], 1.0 / NODES, EPS, ALU.mult, ALU.add))
                yield
                eng.wait_ge(s_act, n_act)
                link(v.reciprocal(st[0:n, 4:5], st[0:n, 3:4]))
                link(v.tensor_tensor(st[0:n, 4:5], st[0:n, 4:5], bn[0:n, 0:1], ALU.mult))
                link(v.tensor_scalar(acc[0:n, 0:width], acc[0:n, 0:width], st[0:n, 4:5], bn[0:n, 1:2], ALU.mult, ALU.add))
                yield
            stage = batch_norm(M1, LO4, 5, 2, Q_PAD4, Q_ISS, bn0_s, 1)
            for name, value in (("sum", NODE_SUM1), ("sq", NODE_SQ1), ("var", NODE_VAR1), ("bn", NODE_BN1)):
                next(stage)
                at(name, value)
                if name == "sum":
                    link(v.tensor_scalar(cdt[:, :], PS[:, CNT, 0:LO16], 1.0, None, ALU.max))
                    link(v.reciprocal(cdt[:, :], cdt[:, :]))
            eng.wait_ge(s_pe, 5)
            r2v = r2[:, :, 0:FT - NREL].rearrange("p (h c) f -> p c h f", h=4)
            for c in range(C4):
                link(v.tensor_copy(r2v[:, c], PS[0:CH, c // 4, (c % 4) * M1:(c % 4 + 1) * M1]
                                   .rearrange("p (h f) -> p h f", h=4)[:, :, 0:F1 - 1]))
            r2c = r2[:, :, FT - NREL:FT].rearrange("p (h c) f -> p c h f", h=16)
            for c in range(C16):
                link(v.tensor_copy(r2c[:, c], PS[0:CH, 2, c * P:(c + 1) * P].rearrange("p (h f) -> p h f", h=16)))
            link(v.tensor_copy(rec[:, 0:LO8], PS[:, 7, 0:LO8]))
            at("rows1", NODE_ROWS1)
            later_arrays()
            eng.wait_ge(s_rt, 4)

            def gathered2(g, b):
                eng.wait_ge(s_gat[1][b], 16 * TILE_G * turn(g, b))
                rv = rows[b][:, :].rearrange("p (t f) -> p t f", f=RT)
                v.tensor_tensor(uvec[:, :, :, :], rv[:, :, NV + NS:NV + NS + 3 * NV].rearrange("p t (j c) -> p t j c", c=3),
                                sh[:, tiles(g), :].unsqueeze(2).broadcast_to([P, TILE_G, NV, 3]), ALU.mult).then_inc(s_u, 1)
                v.tensor_tensor(tval[:, :, :], tsel[:, tiles(g), :], rv[:, :, RT - NREL:RT], ALU.mult).then_inc(s_t, 1)

            def gathered2_sums(g, b):
                rv = rows[b][:, :].rearrange("p (t f) -> p t f", f=RT)
                eng.wait_ge(s_u, 2 * g + 1)
                v.tensor_reduce(rv[:, :, 0:NV], uvec[:, :, :, :], AX, ALU.add).then_inc(s_u, 1)
                eng.wait_ge(s_t, 2 * g + 1)
                v.tensor_reduce(we[:, tiles(g)], tval[:, :, :], AX, ALU.add).then_inc(s_t, 1)

            def pass2(g, b):
                if not first(g, 1):
                    first_rest(1, g - 1, 1 - b)
                eng.wait_ge(s_u, 2 * g + 2)
                xg = rows[b][:, :].rearrange("p (t f) -> p t f", f=RT)[:, :, 0:NV + NS]
                mv = msg[b][:, 0:TILE_G * NS].rearrange("p (t f) -> p t f", f=NS)
                for h in range(2):
                    products(1, g, h, xg, NS, NV + NS)
                if not first(g, 1):
                    second_rest(1, g - 1, 1 - b)
                for h in range(2):
                    eng.wait_ge(s_prod[1], 2 * g + 1 + h)
                    pv = prod[:, h, :].rearrange("p (t j i) -> p t j i", t=2, j=NS)
                    last = v.tensor_reduce(mv[:, 2 * h:2 * h + 2, :], pv, AX, ALU.add)
                last.then_inc(s_red[1], 1)
                if not last_group(g):
                    gathered2(g + 1, 1 - b)
                if not first(g, 1):
                    stack(1, g - 1, 1 - b, [0])
                if not last_group(g):
                    gathered2_sums(g + 1, 1 - b)
                if not first(g, 1):
                    stack(1, g - 1, 1 - b, [1, 2])
            gathered2(0, 0)
            gathered2_sums(0, 0)
            pipelined(eng, pass2)
            finish(1)

            eng.wait_ge(s_scat[1], 1 + GROUPS)
            link(v.scalar_tensor_tensor(acc[:, 0:LO8], PS[:, ACC, 0:LO8], (NS + NV) ** -0.5, rec[:, 0:LO8],
                                        ALU.mult, ALU.mult))
            stage = batch_norm(P, LO8, 5, 6, Q_PAD8, None, bn1_s, 2)
            for name, value in (("sum", NODE_SUM2), ("sq", NODE_SQ2), ("var", NODE_VAR2), ("bn", NODE_BN2)):
                next(stage)
                at(name, value)

            def layer_norm(bank, plus, to, n_act):
                d = lnd[:, :, :].rearrange("p q f -> p (q f)")
                link(v.tensor_tensor(to[:, :, :].rearrange("p c n -> p (c n)"), PS[0:CH, bank, :],
                                     plus[:, :, :].rearrange("p c n -> p (c n)"), ALU.add))
                tv = to[:, :, :].rearrange("p c (h f) -> p (c h) f", f=NS)
                wide = [CH, NQ, NS]
                link(v.tensor_reduce(lnm[:, :], tv, AX, ALU.add))
                link(v.tensor_scalar(lnm[:, :], lnm[:, :], 1.0 / NS, None, ALU.mult))
                link(v.tensor_tensor(tv, tv, lnm[:, :].unsqueeze(2).broadcast_to(wide), ALU.subtract))
                link(v.tensor_tensor(lnd[:, :, :], tv, tv, ALU.mult))
                link(v.tensor_reduce(lnv[:, :], lnd[:, :, :], AX, ALU.add))
                link(v.tensor_scalar(lnv[:, :], lnv[:, :], 1.0 / NS, EPS, ALU.mult, ALU.add))
                yield
                eng.wait_ge(s_act, n_act)
                link(v.reciprocal(lnr[:, :], lnr[:, :]))
                link(v.tensor_tensor(tv, tv, lnr[:, :].unsqueeze(2).broadcast_to(wide), ALU.mult))
                yield
            eng.wait_ge(s_pe, 8)
            eng.wait_ge(s_x, 16 * C8)
            stage = layer_norm(2, xr, x1, 3)
            next(stage)
            at("ln1", NODE_LN1)
            next(stage)
            at("x1", NODE_X1)
            eng.wait_ge(s_pe, 9)
            link(v.tensor_copy(x1t[:, :], PS[:, 3, 0:LO8]))
            at("x1t", NODE_X1T)
            y1v = ysb[0:CH, :].rearrange("p (n m) -> p n m", m=512)
            for n in range(0, 4 * C8, 2):
                eng.wait_ge(s_pe, 10 + n)
                v.tensor_copy(y1v[:, n, :], PS[0:CH, 4 + n % 4, :]).then_inc(s_ysb, 1)

            def relational(n):
                f = MESSAGE[n]

                def step(g, b):
                    eng.wait_ge(s_gat[n][b], 16 * TILE_G * turn(g, b))
                    v.tensor_tensor(msg[b][:, 0:TILE_G * f].rearrange("p (t f) -> p t f", f=f),
                                    rows[b][:, 0:TILE_G * f].rearrange("p (t f) -> p t f", f=f),
                                    we[:, tiles(g)].unsqueeze(2).broadcast_to([P, TILE_G, f]), ALU.mult).then_inc(s_red[n], 1)
                    if not first(g, 1):
                        first_rest(n, g - 1, 1 - b)
                        second_rest(n, g - 1, 1 - b)
                        stack(n, g - 1, 1 - b)
                groups(eng, step)
                finish(n)
            relational(2)
            eng.wait_ge(s_tab, 16 * (1 + C8))
            for n in range(0, C4, 2):
                eng.wait_ge(s_pe, 10 + 4 * C8 + n)
                v.tensor_copy(y1v[:, n, :], PS[0:CH, 4 + n % 4, :]).then_inc(s_ysb, 1)
            relational(3)
            eng.wait_ge(s_scat[3], 1 + GROUPS)
            link(v.tensor_scalar(acc[:, 0:LO8], PS[:, 2, 0:LO8], rb2_s[:, 0:1], None, ALU.add))
            at("b2", NODE_B2)
            eng.wait_ge(s_pe, PE_OUT)
            stage = layer_norm(3, x1, x2, 5)
            next(stage)
            at("ln2", NODE_LN2)
            next(stage)
            at("out", NODE_OUT)


NODE_SUM1 = 8
NODE_SQ1 = NODE_SUM1 + 2 + 5
NODE_VAR1 = NODE_SQ1 + 1
NODE_BN1 = NODE_VAR1 + 3
NODE_ROWS1 = NODE_BN1 + C4 + C16 + 1
NODE_SUM2 = NODE_ROWS1 + 3
NODE_SQ2 = NODE_SUM2 + 5
NODE_VAR2 = NODE_SQ2 + 1
NODE_BN2 = NODE_VAR2 + 3
NODE_LN1 = NODE_BN2 + 7
NODE_X1 = NODE_LN1 + 2
NODE_X1T = NODE_X1 + 1
NODE_B2 = NODE_X1T + 1
NODE_LN2 = NODE_B2 + 7
NODE_OUT = NODE_LN2 + 2
ACT_H = 4
PE_OUT = 9 + 4 * C8 + C4 + 1


def _constants(np):
    row = np.concatenate([np.arange(LO4), np.repeat(np.arange(4), F1), np.repeat(np.arange(4), HID),
                          np.repeat(np.arange(8), NS)])
    c16 = np.ascontiguousarray(np.broadcast_to(row.astype(np.float16), (P, K_END)))
    c32 = np.zeros((P, Q_END), np.float32)
    q, m = np.arange(M1)[:, None], np.arange(M1)[None, :]
    qf, mf = q % F1, m % F1
    c32[:, Q_ID:Q_ID + P] = np.eye(P)
    c32[:M1, Q_CNT:Q_CNT + M1] = (qf == F1 - 1) & (q // F1 == m // F1)
    c32[:M1, Q_SUM:Q_SUM + M1] = qf == mf
    both = (qf >= NS) & (mf >= NS) & (qf < F1 - 1) & (mf < F1 - 1) & ((qf - NS) // 3 == (mf - NS) // 3)
    c32[:M1, Q_SQ:Q_SQ + M1] = np.where(qf < NS, qf == mf, both / 3)
    wide = np.arange(P)[None, :]
    for b in range(2):
        c32[:M1, Q_B0 + b * P:Q_B0 + (b + 1) * P] = (qf == F1 - 1) & (wide // NS == 2 * (q // F1) + b)
    c32[:, Q_S16:Q_S16 + P] = np.arange(P)[:, None] % NS == wide % NS
    c32[:M1, Q_PAD4] = np.arange(M1) // F1 < 3
    c32[:M1, Q_ISS] = np.arange(M1) % F1 < NS
    c32[:, Q_PAD8] = np.arange(P) // NS < 7
    return c16, c32


def kernel(**inputs):
    import numpy as np
    import concourse.bacc as bacc
    from concourse.bass_utils import run_bass_kernel_spmd

    a = {n: np.asarray(v) for n, v in inputs.items()}
    slots = TILES * P

    def edges(v, fill):
        full = np.full((slots,) + v.shape[1:], fill, v.dtype)
        full[:EDGES] = v
        return np.ascontiguousarray(full.reshape((TILES, P) + v.shape[1:]).swapaxes(0, 1))

    x = np.zeros((NPAD, NS), np.float32)
    x[:NODES] = a["x"]
    attr = np.zeros((FD, slots), np.float32)
    attr[:, :EDGES] = a["edge_attr_48"].T
    w1 = np.zeros((FD, H1AT + HROWS), np.float32)
    fcb = np.zeros((H1AT + HROWS, 1), np.float32)
    for n, at in ((0, 0), (1, H1AT)):
        w1[:, at:at + FD] = a[f"L0_gnn_fc{n}_w1"]
        fcb[at:at + FD, 0] = a[f"L0_gnn_fc{n}_b1"]
        fcb[at + FD, 0] = 1

    def weights(n):
        w = np.concatenate([a[f"L0_gnn_fc{n}_w2"], a[f"L0_gnn_fc{n}_b2"][None]])
        s, v = w[:, :NS * NS].reshape(HROWS, NS, NS), w[:, NS * NS:]
        if n == 0:
            w = np.concatenate([v.reshape(HROWS, NS, NV), s], 2)
        else:
            w = np.concatenate([v.reshape(HROWS, NV, NS), s], 1)
        return np.ascontiguousarray(w.transpose(0, 2, 1).reshape(HROWS, NW1))

    bn0 = np.zeros((4, F1, 2), np.float32)
    bn0[:, :NS, 0], bn0[:, :NS, 1] = a["L0_gnn_bn0_gs"], a["L0_gnn_bn0_bs"]
    bn0[:, NS:F1 - 1, 0] = np.repeat(a["L0_gnn_bn0_gv"], 3)
    bn1 = np.tile(np.stack([a["L0_gnn_bn1_gs"], a["L0_gnn_bn1_bs"]], 1), (8, 1))
    c16, c32 = _constants(np)
    arrays = {
        "x": x, "dst": edges(a["dst"], NODES), "src": edges(a["src"], NODES), "typ": edges(a["edge_type_8"], 0),
        "attr": attr, "vec": edges(a["edge_attr_3"], 0), "w1": w1, "fcb": fcb, "w2a": weights(0), "w2b": weights(1),
        "bn0": bn0.reshape(M1, 2), "bn1": bn1,
        "rw1": np.ascontiguousarray(a["L1_gnn_W1"].transpose(1, 0, 2).reshape(NS, NREL * HID)),
        "rr1": a["L1_gnn_root1"], "rb1": np.tile(a["L1_gnn_b1"], 4)[:, None],
        "rw2": np.ascontiguousarray(a["L1_gnn_W2"].transpose(1, 0, 2).reshape(HID, NREL * NS)),
        "rr2": a["L1_gnn_root2"], "rb2": np.tile(a["L1_gnn_b2"], 8)[:, None], "cst16": c16, "cst32": c32,
    }
    nc = bacc.Bacc("TRN2", target_bir_lowering=False, num_devices=1)
    arrays = {f"in_{n}": np.ascontiguousarray(v) for n, v in arrays.items()}
    args = [nc.dram_tensor(n, v.shape, mybir.dt.from_np(v.dtype), kind="ExternalInput").ap() for n, v in arrays.items()]
    out = nc.dram_tensor("out", (NPAD, NS), mybir.dt.float32, kind="ExternalOutput").ap()
    gnn_kernel(nc, *args, out)
    r = run_bass_kernel_spmd(nc, [arrays], core_ids=[0])
    return np.ascontiguousarray(r.results[0]["out"][:NODES])
```
